# Optimizing a Trainium2 kernel written in Bass

```python
import numpy as np
import jax
import jax.numpy as jnp

def _softmax(x, axis=-1):
    return jax.nn.softmax(x, axis=axis)

def _gelu(x):
    return jax.nn.gelu(x, approximate=True)

def _silu(x):
    return jax.nn.silu(x)

def _sigmoid(x):
    return jax.nn.sigmoid(x)

def _layernorm(x, axis=-1, eps=1e-05):
    m = jnp.mean(x, axis=axis, keepdims=True)
    v = jnp.var(x, axis=axis, keepdims=True)
    return (x - m) / jnp.sqrt(v + eps)

def _scatter_add(tgt, idx, src, axis=0):
    return tgt.at[idx].add(src)

def _segment_sum(src, seg, n):
    return jax.ops.segment_sum(src, seg, n)
kernel_name = 'mk_cond_resid_d4_seqx_r4_804f51'

def setup_inputs(seed: int=0):
    np.random.seed(seed)
    _w = jnp.asarray

    def _rec_inputs():
        import jax
        import jax.numpy as jnp
        _rk = jax.random.key(seed)
        x = -7.109e-05 + 0.9999 * jax.random.normal(jax.random.fold_in(_rk, 1), (128, 64, 1024), jnp.float32)
        _lenS = 64 - jax.random.randint(jax.random.fold_in(_rk, 7), (128,), 0, max(1, 64 // 4) + 1, jnp.int32)
        _lenS2 = 64 - jax.random.randint(jax.random.fold_in(_rk, 8), (128,), 0, max(1, 64 // 4) + 1, jnp.int32)
        itok_B_0_15 = jax.random.randint(jax.random.fold_in(_rk, 11), (128,), 0, 16, jnp.int32)
        itok_B_78_3631 = jax.random.randint(jax.random.fold_in(_rk, 12), (128,), 78, 908, jnp.int32)
        itok_B_1_7 = jax.random.randint(jax.random.fold_in(_rk, 13), (128,), 1, 8, jnp.int32)
        itok_B_8_3872 = jax.random.randint(jax.random.fold_in(_rk, 14), (128,), 8, 3873, jnp.int32)
        return (x, itok_B_0_15, itok_B_78_3631, itok_B_1_7, itok_B_8_3872)
    x, itok_B_0_15, itok_B_78_3631, itok_B_1_7, itok_B_8_3872 = _rec_inputs()

    def _L0_cond_setup():
        import jax, jax.numpy as jnp
        import numpy as np
        NUM_CONDITIONS = 16
        IN_CH = 64
        OUT_CH = 64
        B = 64
        T = 1024
        key = jax.random.key(seed)
        k_x, k_w, k_c = jax.random.split(key, 3)
        x = jax.random.normal(k_x, (B, IN_CH, T), dtype=jnp.float32)
        bound = float(np.sqrt(6.0 / IN_CH))
        weights = jax.random.uniform(k_w, (NUM_CONDITIONS, IN_CH, OUT_CH), dtype=jnp.float32, minval=-bound, maxval=bound)
        condition = jax.random.randint(k_c, (B,), 0, NUM_CONDITIONS, dtype=jnp.int64)
        return {'x': x, 'weights': weights, 'condition': condition}
    _L0_cond_all = _L0_cond_setup()
    _L0_cond_in = {k: v for k, v in _L0_cond_all.items() if k in ('weights',)}
    del _L0_cond_all

    def _L1_cond_setup():
        import math
        import jax, jax.numpy as jnp
        import numpy as np
        B, H, N, L = (16, 64, 64, 1024)
        DT_MIN, DT_MAX = (0.001, 0.1)

        def _get_kernel(log_dt, C, log_A_real, A_imag, length):
            dt = jnp.exp(log_dt)
            Cc = C[..., 0] + 1j * C[..., 1]
            A = -jnp.exp(log_A_real) + 1j * A_imag
            dtA = A * dt[:, None]
            Ct = Cc * (jnp.exp(dtA) - 1.0) / A
            P = dtA[:, :, None] * jnp.arange(length, dtype=jnp.float32)
            K = 2.0 * jnp.einsum('hn,hnl->hl', Ct, jnp.exp(P)).real
            return K
        key = jax.random.key(seed)
        ks = jax.random.split(key, 5)
        u = jax.random.normal(ks[0], (B, H, L), dtype=jnp.float32)
        log_dt = jax.random.uniform(ks[1], (H,), dtype=jnp.float32) * (math.log(DT_MAX) - math.log(DT_MIN)) + math.log(DT_MIN)
        C = jax.random.normal(ks[2], (H, N, 2), dtype=jnp.float32)
        log_A_real = jnp.log(0.5 * jnp.ones((H, N), dtype=jnp.float32))
        A_imag = math.pi * jnp.broadcast_to(jnp.arange(N, dtype=jnp.float32), (H, N))
        D = jax.random.normal(ks[3], (H,), dtype=jnp.float32)
        length = jax.random.randint(ks[4], (B,), 1, L + 1, dtype=jnp.int32)
        return {'u': u, 'log_dt': log_dt, 'C': C, 'log_A_real': log_A_real, 'A_imag': A_imag, 'D': D, 'length': length}
    _L1_cond_all = _L1_cond_setup()
    _L1_cond_in = {k: v for k, v in _L1_cond_all.items() if k in ('log_dt', 'C', 'log_A_real', 'A_imag', 'D')}
    del _L1_cond_all

    def _L2_cond_setup():
        import jax, jax.numpy as jnp
        import numpy as np
        B, S, D_IN, D_OUT = (4, 512, 1024, 1024)
        N_ADAPTERS, MAX_RANK = (8, 16)
        key = jax.random.key(seed)
        ks = jax.random.split(key, 7)
        x = jax.random.normal(ks[0], (B, S, D_IN), dtype=jnp.float32)
        weight = jax.random.normal(ks[1], (D_OUT, D_IN), dtype=jnp.float32) * (1.0 / np.sqrt(D_IN))
        bias = jax.random.normal(ks[2], (D_OUT,), dtype=jnp.float32) * 0.01
        lora_a_weights = jax.random.normal(ks[3], (N_ADAPTERS, MAX_RANK, D_IN), dtype=jnp.float32) * (1.0 / np.sqrt(D_IN))
        lora_b_weights = jax.random.normal(ks[4], (N_ADAPTERS, D_OUT, MAX_RANK), dtype=jnp.float32) * 0.02
        scaling_factors = jax.random.uniform(ks[5], (N_ADAPTERS,), dtype=jnp.float32, minval=0.5, maxval=2.0)
        adapter_id = jax.random.randint(ks[6], (B,), 0, N_ADAPTERS, dtype=jnp.int64)
        return {'x': x, 'weight': weight, 'bias': bias, 'lora_a_weights': lora_a_weights, 'lora_b_weights': lora_b_weights, 'scaling_factors': scaling_factors, 'adapter_id': adapter_id}
    _L2_cond_all = _L2_cond_setup()
    _L2_cond_in = {k: v for k, v in _L2_cond_all.items() if k in ('weight', 'bias', 'lora_a_weights', 'lora_b_weights', 'scaling_factors')}
    del _L2_cond_all

    def _L3_cond_setup():
        import math
        import jax, jax.numpy as jnp
        import numpy as np
        H, N, B, L = (64, 64, 16, 1024)
        DT_MIN, DT_MAX = (0.001, 0.1)

        def _get_kernel(log_dt, C, log_A_real, A_imag, length):
            Cc = C[..., 0] + 1j * C[..., 1]
            dt = jnp.exp(log_dt)
            A = -jnp.exp(log_A_real) + 1j * A_imag
            dtA = A * dt[:, None]
            P = dtA[:, :, None] * jnp.arange(length, dtype=jnp.float32)
            Cs = Cc * (jnp.exp(dtA) - 1.0) / A
            K = 2.0 * jnp.einsum('hn,hnl->hl', Cs, jnp.exp(P)).real
            return K
        key = jax.random.key(seed)
        ks = jax.random.split(key, 6)
        u = jax.random.normal(ks[0], (B, H, L), dtype=jnp.float32)
        length = jax.random.randint(ks[1], (B,), 0, L)
        log_dt = jax.random.uniform(ks[2], (H,), dtype=jnp.float32) * (math.log(DT_MAX) - math.log(DT_MIN)) + math.log(DT_MIN)
        C = jax.random.normal(ks[3], (H, N, 2), dtype=jnp.float32)
        log_A_real = jnp.log(0.5 * jnp.ones((H, N), dtype=jnp.float32))
        A_imag = math.pi * jnp.broadcast_to(jnp.arange(N, dtype=jnp.float32), (H, N))
        D = jax.random.normal(ks[4], (H,), dtype=jnp.float32)
        return {'u': u, 'length': length, 'log_dt': log_dt, 'C': C, 'log_A_real': log_A_real, 'A_imag': A_imag, 'D': D}
    _L3_cond_all = _L3_cond_setup()
    _L3_cond_in = {k: v for k, v in _L3_cond_all.items() if k in ('log_dt', 'C', 'log_A_real', 'A_imag', 'D')}
    del _L3_cond_all
    return {'x': x, 'itok_B_0_15': itok_B_0_15, 'itok_B_78_3631': itok_B_78_3631, 'itok_B_1_7': itok_B_1_7, 'itok_B_8_3872': itok_B_8_3872, 'L0_cond_weights': _L0_cond_in['weights'], 'L1_cond_log_dt': _L1_cond_in['log_dt'], 'L1_cond_C': _L1_cond_in['C'], 'L1_cond_log_A_real': _L1_cond_in['log_A_real'], 'L1_cond_A_imag': _L1_cond_in['A_imag'], 'L1_cond_D': _L1_cond_in['D'], 'L2_cond_weight': _L2_cond_in['weight'], 'L2_cond_bias': _L2_cond_in['bias'], 'L2_cond_lora_a_weights': _L2_cond_in['lora_a_weights'], 'L2_cond_lora_b_weights': _L2_cond_in['lora_b_weights'], 'L2_cond_scaling_factors': _L2_cond_in['scaling_factors'], 'L3_cond_log_dt': _L3_cond_in['log_dt'], 'L3_cond_C': _L3_cond_in['C'], 'L3_cond_log_A_real': _L3_cond_in['log_A_real'], 'L3_cond_A_imag': _L3_cond_in['A_imag'], 'L3_cond_D': _L3_cond_in['D']}

def reference(x, itok_B_0_15, itok_B_78_3631, itok_B_1_7, itok_B_8_3872, L0_cond_weights, L1_cond_log_dt, L1_cond_C, L1_cond_log_A_real, L1_cond_A_imag, L1_cond_D, L2_cond_weight, L2_cond_bias, L2_cond_lora_a_weights, L2_cond_lora_b_weights, L2_cond_scaling_factors, L3_cond_log_dt, L3_cond_C, L3_cond_log_A_real, L3_cond_A_imag, L3_cond_D):
    import jax
    import jax.numpy as jnp

    def _L0_cond_ref(x, weights, condition):
        import jax, jax.numpy as jnp
        import numpy as np
        NUM_CONDITIONS = 16
        IN_CH = 64
        OUT_CH = 64
        B = 64
        T = 1024
        W = weights[condition]
        return jnp.einsum('bct,bcd->bdt', x, W)

    def _L1_cond_ref(u, log_dt, C, log_A_real, A_imag, D, length):
        import math
        import jax, jax.numpy as jnp
        import numpy as np
        B, H, N, L = (16, 64, 64, 1024)
        DT_MIN, DT_MAX = (0.001, 0.1)

        def _get_kernel(log_dt, C, log_A_real, A_imag, length):
            dt = jnp.exp(log_dt)
            Cc = C[..., 0] + 1j * C[..., 1]
            A = -jnp.exp(log_A_real) + 1j * A_imag
            dtA = A * dt[:, None]
            Ct = Cc * (jnp.exp(dtA) - 1.0) / A
            P = dtA[:, :, None] * jnp.arange(length, dtype=jnp.float32)
            K = 2.0 * jnp.einsum('hn,hnl->hl', Ct, jnp.exp(P)).real
            return K
        Bq, Hq, Lq = u.shape
        K = _get_kernel(log_dt, C, log_A_real, A_imag, Lq)
        n = 2 * Lq
        kf = jnp.fft.rfft(K, n=n)
        uf = jnp.fft.rfft(u, n=n)
        y = jnp.fft.irfft(uf * kf[None], n=n)[..., :Lq]
        y = y + u * D[:, None]
        mask = (jnp.arange(Lq)[None, :] < length[:, None]).astype(u.dtype)
        return y * mask[:, None, :]

    def _L2_cond_ref(x, weight, bias, lora_a_weights, lora_b_weights, scaling_factors, adapter_id):
        import jax, jax.numpy as jnp
        import numpy as np
        B, S, D_IN, D_OUT = (4, 512, 1024, 1024)
        N_ADAPTERS, MAX_RANK = (8, 16)
        base = jnp.einsum('bsi,oi->bso', x, weight) + bias
        a_sel = lora_a_weights[adapter_id]
        b_sel = lora_b_weights[adapter_id]
        scale = scaling_factors[adapter_id]
        low = jnp.einsum('bsi,bri->bsr', x, a_sel)
        delta = jnp.einsum('bsr,bor->bso', low, b_sel)
        return base + scale[:, None, None] * delta

    def _L3_cond_ref(u, length, log_dt, C, log_A_real, A_imag, D):
        import math
        import jax, jax.numpy as jnp
        import numpy as np
        H, N, B, L = (64, 64, 16, 1024)
        DT_MIN, DT_MAX = (0.001, 0.1)

        def _get_kernel(log_dt, C, log_A_real, A_imag, length):
            Cc = C[..., 0] + 1j * C[..., 1]
            dt = jnp.exp(log_dt)
            A = -jnp.exp(log_A_real) + 1j * A_imag
            dtA = A * dt[:, None]
            P = dtA[:, :, None] * jnp.arange(length, dtype=jnp.float32)
            Cs = Cc * (jnp.exp(dtA) - 1.0) / A
            K = 2.0 * jnp.einsum('hn,hnl->hl', Cs, jnp.exp(P)).real
            return K
        Bq, Hq, Lq = u.shape
        mask = (jnp.arange(Lq) < length[:, None]).astype(u.dtype)
        u_m = u * mask[:, None, :]
        kernel = _get_kernel(log_dt, C, log_A_real, A_imag, Lq)
        n = 2 * Lq
        k_f = jnp.fft.rfft(kernel, n=n)
        u_f = jnp.fft.rfft(u_m, n=n)
        y = jnp.fft.irfft(u_f * k_f, n=n)[..., :Lq]
        y = y + u_m * D[:, None]
        return y * mask[:, None, :]
    x = x + _L0_cond_ref(x, L0_cond_weights, itok_B_0_15)
    x = x + _L1_cond_ref(x, L1_cond_log_dt, L1_cond_C, L1_cond_log_A_real, L1_cond_A_imag, L1_cond_D, itok_B_78_3631)
    x = x + _L2_cond_ref(x, L2_cond_weight, L2_cond_bias, L2_cond_lora_a_weights, L2_cond_lora_b_weights, L2_cond_scaling_factors, itok_B_1_7)
    x = x + _L3_cond_ref(x, itok_B_8_3872, L3_cond_log_dt, L3_cond_C, L3_cond_log_A_real, L3_cond_A_imag, L3_cond_D)
    return x

_drawn_inputs = setup_inputs


def setup_inputs(seed=0):
    import zlib

    import numpy as np

    out = dict(_drawn_inputs(seed))
    spreads = {'L1_cond_log_A_real': (-0.6931471824645996, 0.2),
     'L3_cond_log_A_real': (-0.6931471824645996, 0.2)}
    factors = {'L2_cond_bias': 8.0}
    for name, (base, spread) in spreads.items():
        noise = np.random.default_rng([zlib.crc32(name.encode()), seed]).standard_normal(out[name].shape)
        drawn = base * np.exp(spread * noise) if base else spread * noise
        out[name] = jnp.asarray(drawn.astype(out[name].dtype))
    for name, factor in factors.items():
        out[name] = (out[name] * factor).astype(out[name].dtype)
    return out
```

```python
import math
from contextlib import ExitStack

import concourse.bass as bass
from concourse import mybir

ALU = mybir.AluOpType
ACT = mybir.ActivationFunctionType
F32 = mybir.dt.float32
F16 = mybir.dt.float16
I32 = mybir.dt.int32
U8 = mybir.dt.uint8

P = 128
B, C, T = 128, 64, 1024
NBLK = T // P
NID, NADAPT, RANK = 16, 8, 16
NMODE = 64
XS, WS = 32.0, 64.0
FS = XS * WS
PAIRS = B // 2
GPAIRS = 8
STEPS = PAIRS // GPAIRS
HG = 4
NG = C // HG
COLS = HG * B
TB = 32
KROW = P + T

ROUND = 12582912.0
TWO_PI_HI = 6.28125
TWO_PI_LO = 2 * math.pi - TWO_PI_HI
LN2_HI = 0.693359375
LN2_LO = math.log(2.0) - LN2_HI
PI_CLAMP = 3.1415925


def at_least(engine, semaphore, value):
    if not (isinstance(value, int) and value <= 0):
        engine.wait_ge(semaphore, value)


def build(nc, x, ids0, len1, ids2, len3, w0, ssm1, ssm3, w2, bias2, lora_a, lora_b, lora_s, out):
    with ExitStack() as ctx:
        def sem(name):
            return ctx.enter_context(nc.semaphore(name))

        def sb(name, shape, dt):
            return ctx.enter_context(nc.sbuf_tensor(name, shape, dt))

        x1_dram = nc.dram_tensor("x1_scratch", [NBLK, P, C, B], F32).ap()
        krow_t = nc.dram_tensor("krow_scratch", [2, C, 2, KROW], F16)
        krow = krow_t.ap()

        ps = ctx.enter_context(nc.psum_tensor("ps", [P, 8, 512], F32))

        ident = sb("ident", [P, P], F32)
        w2t = sb("w2t", [P, 2, NBLK, T], F16)
        at = sb("at", [P, 2, NBLK, P], F16)
        bt = sb("bt", [P, 2, T], F16)
        adapter_scale = sb("adapter_scale", [P, B], F32)
        biasx = sb("biasx", [P, NBLK], F32)
        mask1 = sb("mask1", [P, NBLK, B], U8)
        past3 = sb("past3", [P, T], U8)
        flip = sb("flip", [P, P], F16)
        g1n = sb("g1n", [P, 2, 2, T], F16)
        g1 = sb("g1", [P, HG, 2, T], F16)
        g3 = sb("g3", [P, HG, 2, T], F16)
        small = sb("small", [P, 64], F32)
        d_row = sb("d_row", [1, 2 * C], F32)

        ARENA = 120 * 256
        arena = sb("arena", [P, ARENA], F32)

        def area(at_kb, kb, dt=F32):
            v = arena[:, at_kb * 256:(at_kb + kb) * 256]
            return v if dt == F32 else v.bitcast(dt)

        prm = area(0, 32)
        tabs = [area(32 + 8 * n, 8) for n in range(10)]
        pick = area(0, 32, F16).rearrange("p (n s d) -> p n s d", n=PAIRS, s=2)
        xin = area(32, 16).rearrange("p (s n t) -> p s n t", s=4, n=GPAIRS)
        xh = area(48, 4, F16).rearrange("p (s n t) -> p s n t", s=2, n=GPAIRS)
        xl = area(52, 4, F16).rearrange("p (s n t) -> p s n t", s=2, n=GPAIRS)
        xq = area(56, 64).rearrange("p (k d b) -> p k d b", k=2, d=C)
        w0n = area(56, 16)
        w0s = area(72, 16)
        w0h = area(88, 8, F16)
        w0l = area(96, 8, F16)
        w2n = area(0, 32).rearrange("p (k i) -> p k i", k=NBLK)
        an = area(32, 4)
        bn = area(36, 4)
        w2r = area(40, 32).rearrange("p (k i) -> p k i", k=NBLK)
        a_rev = area(72, 4)
        x1f = area(0, 16).rearrange("p (h k b) -> p h k b", h=HG, k=NBLK)
        x1h = area(16, 8, F16).rearrange("p (h k b) -> p h k b", h=HG, k=NBLK)
        x1l = area(24, 8, F16).rearrange("p (h k b) -> p h k b", h=HG, k=NBLK)
        x2h = area(32, 8, F16).rearrange("p (h k b) -> p h k b", h=HG, k=NBLK)
        x2l = area(40, 8, F16).rearrange("p (h k b) -> p h k b", h=HG, k=NBLK)
        x3h = area(48, 8, F16).rearrange("p (h k b) -> p h k b", h=HG, k=NBLK)
        x3l = area(56, 8, F16).rearrange("p (h k b) -> p h k b", h=HG, k=NBLK)
        outt = area(64, 16).rearrange("p (h t) -> p h t", h=HG)
        x3f = area(80, 4).rearrange("p (s h b) -> p s h b", s=2, h=HG)
        lowf = area(84, 2).rearrange("p (h b) -> p h b", h=HG)
        lowh = area(86, 1, F16)
        lowl = area(87, 1, F16)

        pcol = small[:, 0:1]
        phase_own = small[:, 1:2]
        phase_oth = small[:, 2:3]
        turn_own = small[:, 3:4]
        turn_oth = small[:, 4:5]
        rank_scale = small[:, 5:6]
        rank_adapter = small[:, 6:7]
        len3f = small[:, 7:8]
        len3i = small[:, 8:9].bitcast(I32)
        pcoli = small[:, 9:10].bitcast(I32)
        tcol = small[:, 16:24]
        tcoli = small[:, 24:32].bitcast(I32)
        biasn = tabs[8][:, T:T + P]
        bias_rev = tabs[8][:, T + P:T + 2 * P]
        ids = sb("ids", [P, 3, B], I32)
        idf = sb("idf", [P, 3, B], F32)
        onehot = sb("onehot", [NID, B], F16)
        trow = tabs[9]
        trowi = tabs[8].bitcast(I32)

        consts_loaded = sem("consts_loaded")
        iota_done = sem("iota_done")
        ids_loaded = sem("ids_loaded")
        w0_loaded = sem("w0_loaded")
        ssm_loaded = sem("ssm_loaded")
        dve_step = sem("dve_step")
        act_step = sem("act_step")
        masks_ready = sem("masks_ready")
        params_ready = sem("params_ready")
        params_turned = sem("params_turned")
        turned_copied = sem("turned_copied")
        angles_ready = sem("angles_ready")
        sines_ready = sem("sines_ready")
        tables_ready = sem("tables_ready")
        k_summed = sem("k_summed")
        k_scaled = sem("k_scaled")
        k_split = sem("k_split")
        krow_stored = sem("krow_stored")
        zeros_ready = sem("zeros_ready")
        w0_split = sem("w0_split")
        pick_cleared = sem("pick_cleared")
        pick_summed = sem("pick_summed")
        pick_hi_copied = sem("pick_hi_copied")
        pick_lo_copied = sem("pick_lo_copied")
        x_loaded = [sem(f"x_loaded{s}") for s in range(4)]
        x_hi = sem("x_hi")
        x_lo = sem("x_lo")
        s0_summed = sem("s0_summed")
        s0_left_out = sem("s0_left_out")
        s0_right_out = sem("s0_right_out")
        x1_stored = [sem(f"x1_stored{k}") for k in range(2)]
        w2_loaded = sem("w2_loaded")
        w2_ready = sem("w2_ready")
        w2_turned = sem("w2_turned")
        w2_hi = sem("w2_hi")
        w2_lo = sem("w2_lo")
        x1_loaded = [sem(f"x1_loaded{h}") for h in range(HG)]
        g1_loaded = [sem(f"g1_loaded{h}") for h in range(HG)]
        g3_loaded = [sem(f"g3_loaded{h}") for h in range(HG)]
        out_stored = [sem(f"out_stored{h}") for h in range(HG)]
        x1_hi = sem("x1_hi")
        x1_lo = sem("x1_lo")
        g1_turned = sem("g1_turned")
        c1_summed = sem("c1_summed")
        c1_out = sem("c1_out")
        x2_hi = sem("x2_hi")
        x2_lo = sem("x2_lo")
        low_summed = sem("low_summed")
        low_scaled = sem("low_scaled")
        low_hi = sem("low_hi")
        low_lo = sem("low_lo")
        s2_summed = sem("s2_summed")
        x3_hi = sem("x3_hi")
        s2_out = sem("s2_out")
        x3_lo = sem("x3_lo")
        c3_summed = sem("c3_summed")
        c3_out = sem("c3_out")
        c3_past = sem("c3_past")

        ssm = (ssm1, ssm3)
        NTURN = 2 * NBLK + 4

        x_pairs = x.rearrange("(n q) c t -> (q c) n t", q=2)

        def turned_source(n):
            if n < 2 * NBLK:
                k, half = n // 2, n % 2
                return [w2r[:, 4 * half + m, k * P:(k + 1) * P] for m in range(4)]
            if n < 2 * NBLK + 2:
                return [a_rev[:, (4 * (n - 2 * NBLK) + m) * P:][:, 0:P] for m in range(4)]
            return [bn[:, (4 * (n - 2 * NBLK - 2) + m) * P:][:, 0:P] for m in range(4)]

        def turned_target(n, part):
            if n < 2 * NBLK:
                k, half = n // 2, n % 2
                return w2t[:, part, k, half * 512:(half + 1) * 512].rearrange("p (m o) -> p m o", m=4)[:, :, ::-1]
            if n < 2 * NBLK + 2:
                m = 4 * (n - 2 * NBLK)
                return at[:, part, m:m + 4, :]
            m = 4 * (n - 2 * NBLK - 2)
            return bt[:, part, m * P:(m + 4) * P].rearrange("p (m o) -> p m o", m=4)[:, :, ::-1]

        block = ctx.enter_context(nc.Block())

        @block.sync
        def _(sp):
            for v in range(2):
                rows = slice(v * C, (v + 1) * C)
                log_dt, cc, log_ar, a_imag, dd = ssm[v]
                sp.dma_start(prm[rows, 0:1], log_dt.rearrange("(h o) -> h o", o=1)).then_inc(ssm_loaded, 16)
                sp.dma_start(prm[rows, 64:128], log_ar).then_inc(ssm_loaded, 16)
                sp.dma_start(prm[rows, 128:192], a_imag).then_inc(ssm_loaded, 16)
                sp.dma_start(prm[rows, 192:320], cc.rearrange("h n r -> h (n r)")).then_inc(ssm_loaded, 16)
                sp.dma_start(prm[0:1, 320 + v * C:320 + (v + 1) * C], dd.rearrange("(o h) -> o h", o=1)).then_inc(ssm_loaded, 16)
            for n, row in enumerate((ids0, len1, ids2)):
                sp.dma_start(ids[:, n, :], row.rearrange("(o b) -> o b", o=1).to_broadcast([P, B])).then_inc(ids_loaded, 16)
            sp.dma_start(len3i, len3.rearrange("(b o) -> b o", o=1)).then_inc(ids_loaded, 16)
            for a in range(NADAPT):
                sp.dma_start(rank_scale[a * RANK:(a + 1) * RANK, :],
                             lora_s[a:a + 1].rearrange("(o a) -> o a", o=1).to_broadcast([RANK, 1])).then_inc(consts_loaded, 16)
            sp.dma_start(biasn[0:NBLK, :], bias2.rearrange("(k o) -> k o", k=NBLK)).then_inc(consts_loaded, 16)
            sp.wait_ge(zeros_ready, 1)
            sp.dma_start(krow.rearrange("v h s n -> (v h) s n")[:, :, 0:P],
                         tabs[7][:, 0:P].bitcast(F16).rearrange("p (s n) -> p s n", s=2)).then_inc(krow_stored, 16)
            for v in range(2):
                for part in range(2):
                    sp.wait_ge(k_split, 2 * v + part + 1)
                    src = tabs[5 + part][0:TB, v * 1024:(v + 1) * 1024].bitcast(F16).rearrange("a (h b) -> a h b", h=C)
                    dst = krow[v, :, part, P:].rearrange("h (a b) -> a h b", a=TB)
                    sp.dma_start(dst, src).then_inc(krow_stored, 16)
            sp.wait_ge(k_split, 4)
            sp.wait_ge(krow_stored, 80)
            sp.dma_start(w0n[0:NID, :], w0.rearrange("i c d -> i (c d)")).then_inc(w0_loaded, 16)

            def load_x(i, m):
                k, g = m // STEPS, m % STEPS
                n = 2 * STEPS * i + m
                at_least(sp, x_hi, n - 3)
                at_least(sp, x_lo, n - 3)
                t0 = (2 * i + k) * P
                sp.dma_start(xin[:, m % 4], x_pairs[:, g * GPAIRS:(g + 1) * GPAIRS, bass.ds(t0, P)]).then_inc(x_loaded[m % 4], 16)

            def store_x1(i, k):
                sp.wait_ge(s0_left_out, (2 * i + k + 1) * STEPS)
                sp.wait_ge(s0_right_out, (2 * i + k + 1) * STEPS)
                sp.dma_start(x1_dram[bass.ds(2 * i + k, 1)].rearrange("o p d b -> (o p) (d b)"),
                             xq[:, k].rearrange("p d b -> p (d b)")).then_inc(x1_stored[k], 16)

            def stage0(i, first):
                for m in range(2 * STEPS):
                    load_x(i, m)
                    if m == 3 and not first:
                        store_x1(i - 1, 1)
                    if m == STEPS + 3:
                        store_x1(i, 0)

            stage0(0, True)
            with sp.Fori(1, NBLK // 2) as i:
                stage0(i, False)
            store_x1(NBLK // 2 - 1, 1)

            sp.wait_ge(s0_summed, NBLK * STEPS)
            sp.dma_start(w2n, w2.rearrange("(k o) i -> o k i", k=NBLK)).then_inc(w2_loaded, 16)
            sp.dma_start(an, lora_a.rearrange("a r i -> (a r) i")).then_inc(w2_loaded, 16)
            for a in range(NADAPT):
                sp.dma_start(bn.rearrange("p (k a r) -> p k a r", k=NBLK, a=NADAPT)[:, :, a, :],
                             lora_b[a].rearrange("(k o) r -> o k r", k=NBLK)).then_inc(w2_loaded, 16)

            def load_g(v, g, h):
                tile = (g1n[:, h % 2], g3[:, h])[v]
                src = bass.AP(krow_t, (HG * g + h) * (2 * KROW) + v * (C * 2 * KROW) + 1, [[1, P], [KROW, 2], [1, T]])
                sp.dma_start(tile, src).then_inc((g1_loaded, g3_loaded)[v][h], 16)

            def load_x1(g, h):
                src = x1_dram.rearrange("k p d b -> p d k b")[:, bass.ds(HG * g + h, 1)].rearrange("p o k b -> p (o k) b")
                sp.dma_start(x1f[:, h], src).then_inc(x1_loaded[h], 16)

            def load_g1(g, h):
                at_least(sp, g1_turned, HG * g + h - 1)
                load_g(0, g, h)

            for h in range(HG):
                load_g1(0, h)
                load_g(1, 0, h)
            sp.wait_ge(w2_turned, NTURN)
            sp.wait_ge(x1_stored[0], 16 * NBLK // 2)
            sp.wait_ge(x1_stored[1], 16 * NBLK // 2)
            for h in range(HG):
                load_x1(0, h)

            def reload_first(g, h):
                load_g1(g, h)
                sp.wait_ge(x2_hi, HG * (g - 1) + h + 1)
                sp.wait_ge(x2_lo, HG * (g - 1) + h + 1)
                load_x1(g, h)

            for h in range(HG):
                reload_first(1, h)

            def body(g, more1, more2):
                if more2:
                    for h in range(HG):
                        reload_first(g + 2, h)
                for h in range(HG):
                    sp.wait_ge(c3_past, HG * g + h + 1)
                    sp.dma_start(out[:, bass.ds(HG * g + h, 1), :].rearrange("b o t -> b (o t)"), outt[:, h]).then_inc(out_stored[h], 16)
                    if more1:
                        sp.wait_ge(c3_summed, HG * g + h + 1)
                        load_g(1, g + 1, h)

            body(0, True, True)
            with sp.Fori(1, NG - 2) as g:
                body(g, True, True)
            body(NG - 2, True, False)
            body(NG - 1, False, False)
            for h in range(HG):
                sp.wait_ge(out_stored[h], 16 * NG)

        @block.gpsimd
        def _(pool):
            nc.gpsimd.iota(pcoli, [[0, 1]], base=0, channel_multiplier=1).then_inc(iota_done, 1)
            nc.gpsimd.iota(tcoli, [[P, NBLK]], base=P - 1, channel_multiplier=-1).then_inc(iota_done, 1)
            nc.gpsimd.iota(trowi[:, 0:T], [[1, T]], base=0, channel_multiplier=0).then_inc(iota_done, 1)
            nc.gpsimd.memset(ident[:, :], 0.0).then_inc(iota_done, 1)
            nc.gpsimd.memset(flip[:, :], 0.0).then_inc(iota_done, 1)
            pool.wait_ge(iota_done, 5)
            nc.gpsimd.affine_select(out=ident[:, :], in_=ident[:, :], compare_op=ALU.not_equal, fill=1.0, base=0,
                                    pattern=[[-1, P]], channel_multiplier=1).then_inc(iota_done, 1)
            nc.gpsimd.affine_select(out=flip[:, :], in_=flip[:, :], compare_op=ALU.not_equal, fill=1.0 / XS, base=-(P - 1),
                                    pattern=[[1, P]], channel_multiplier=1).then_inc(iota_done, 1)
            nc.gpsimd.memset(tabs[7][:, 0:P], 0.0).then_inc(zeros_ready, 1)
            pool.wait_ge(params_turned, 1)
            nc.gpsimd.memset(area(0, 32), 0.0).then_inc(pick_cleared, 1)

        @block.tensor
        def _(pe):
            pe.wait_ge(params_ready, 1)
            pe.wait_ge(iota_done, 6)
            nc.tensor.transpose(ps[:, 1, 0:NBLK], bias_rev[0:NBLK, :], ident[0:NBLK, 0:NBLK])
            for n in range(4):
                mm = nc.tensor.transpose(ps[:, 0, n * P:(n + 1) * P], prm[:, 1024 + n * P:1024 + (n + 1) * P], ident[:, :])
            mm.then_inc(params_turned, 1)
            for v in range(2):
                pe.wait_ge(tables_ready, v + 1)
                if v:
                    pe.wait_ge(k_scaled, 1)
                for h in range(C):
                    mm = nc.tensor.matmul(ps[0:TB, 1 + h // 16, (h % 16) * TB:(h % 16 + 1) * TB],
                                          tabs[6][:, h * TB:(h + 1) * TB], tabs[5][:, h * TB:(h + 1) * TB], start=True, stop=True)
                mm.then_inc(k_summed, 1)

            pe.wait_ge(w0_split, 2)
            pe.wait_ge(k_scaled, 2)
            for n in range(16):
                dgroup, part = n // 2, n % 2
                at_least(pe, (pick_hi_copied, pick_lo_copied)[part], dgroup - 3)
                src = (w0h, w0l)[part][0:NID, :].rearrange("i (c d) -> i d c", d=C)
                for e in range(8):
                    for q in range(2):
                        mm = nc.tensor.matmul(ps[q * C:(q + 1) * C, n % 8, e * PAIRS:(e + 1) * PAIRS], src[:, 8 * dgroup + e, :],
                                              onehot[:, :].rearrange("i (n q) -> i q n", q=2)[:, q, :], start=True, stop=True)
                mm.then_inc(pick_summed, 1)

            pe.wait_ge(pick_hi_copied, 8)
            pe.wait_ge(pick_lo_copied, 8)

            def stage0(i):
                for m in range(2 * STEPS):
                    n = 2 * STEPS * i + m
                    s = m % 2
                    pe.wait_ge(x_hi, n + 1)
                    pe.wait_ge(x_lo, n + 1)
                    at_least(pe, s0_left_out, n - 3)
                    at_least(pe, s0_right_out, n - 3)
                    for j in range(GPAIRS):
                        o = ps[:, 2 * (m % 4) + j // 4, (j % 4) * P:(j % 4 + 1) * P]
                        w = pick[:, (m % STEPS) * GPAIRS + j]
                        nc.tensor.matmul(o, xh[:, s, j, :], w[:, 0, :], start=True, stop=False)
                        nc.tensor.matmul(o, xh[:, s, j, :], w[:, 1, :], start=False, stop=False)
                        mm = nc.tensor.matmul(o, xl[:, s, j, :], w[:, 0, :], start=False, stop=True)
                    mm.then_inc(s0_summed, 1)

            stage0(0)
            with pe.Fori(1, NBLK // 2) as i:
                stage0(i)

            pe.wait_ge(w2_ready, 1)
            pe.wait_ge(s0_left_out, NBLK * STEPS)
            pe.wait_ge(s0_right_out, NBLK * STEPS)
            for n in range(NTURN):
                at_least(pe, w2_hi, n - 3)
                at_least(pe, w2_lo, n - 3)
                for m, tile in enumerate(turned_source(n)):
                    mm = nc.tensor.transpose(ps[:, n % 4, m * P:(m + 1) * P], tile, ident[:, :])
                mm.then_inc(w2_turned, 1)
            pe.wait_ge(w2_hi, NTURN)
            pe.wait_ge(w2_lo, NTURN)

            def conv1(g, h):
                n = HG * g + h
                b0 = 2 * (h % 2)
                pe.wait_ge(g1_turned, n + 1)
                pe.wait_ge(x1_hi, n + 1)
                pe.wait_ge(x1_lo, n + 1)
                if h < 2:
                    at_least(pe, c3_out, HG * (g - 1))
                else:
                    pe.wait_ge(c1_out, n - 1)
                products = [(0, x1h), (0, x1l), (1, x1h)]
                for d in range(NBLK):
                    for q, (part, xx) in enumerate(products):
                        w = g1[:, h, part, d * P:(d + 1) * P]
                        first, last = d == 0 and q == 0, q == 2
                        if d < 4:
                            nc.tensor.matmul(ps[:, b0, d * B:4 * B], w, xx[:, h, 0:4 - d, :],
                                             start=first, stop=(d == 3 and last))
                        lo = max(0, 4 - d)
                        mm = nc.tensor.matmul(ps[:, b0 + 1, (lo + d - 4) * B:4 * B], w, xx[:, h, lo:NBLK - d, :],
                                              start=first, stop=(d == NBLK - 1 and last))
                mm.then_inc(c1_summed, 1)

            def stage2(g):
                pe.wait_ge(x2_hi, HG * (g + 1))
                pe.wait_ge(x2_lo, HG * (g + 1))
                at_least(pe, c3_past, HG * g)
                products = [(0, x2h), (0, x2l), (1, x2h)]
                for k in range(NBLK):
                    for q, (part, xx) in enumerate(products):
                        mm = nc.tensor.matmul(ps[:, 7, :], at[:, part, k, :], xx[:, :, k, :],
                                              start=(k == 0 and q == 0), stop=(k == NBLK - 1 and q == 2))
                mm.then_inc(low_summed, 1)
                for o in range(NBLK):
                    if o >= 3:
                        pe.wait_ge(s2_out, NBLK * g + o - 2)
                    for k in range(NBLK):
                        for q, (part, xx) in enumerate(products):
                            nc.tensor.matmul(ps[:, 4 + o % 3, :], w2t[:, part, k, o * P:(o + 1) * P], xx[:, :, k, :],
                                             start=(k == 0 and q == 0), stop=False)
                    if o == 0:
                        pe.wait_ge(low_hi, g + 1)
                        pe.wait_ge(low_lo, g + 1)
                    for q, (part, xx) in enumerate([(0, lowh), (0, lowl), (1, lowh)]):
                        mm = nc.tensor.matmul(ps[:, 4 + o % 3, :], bt[:, part, o * P:(o + 1) * P], xx, start=False, stop=(q == 2))
                    mm.then_inc(s2_summed, 1)

            def conv3(g, h):
                n = HG * g + h
                b0, t0 = 2 * (h % 2), 4 + 2 * (h % 2)
                pe.wait_ge(g3_loaded[h], 16 * (g + 1))
                if h == 0:
                    pe.wait_ge(x3_hi, NBLK * (g + 1))
                    pe.wait_ge(x3_lo, NBLK * (g + 1))
                if h < 2:
                    pe.wait_ge(c1_out, conv1_sums_read(g, h))
                else:
                    pe.wait_ge(c3_out, n - 1)
                    pe.wait_ge(c3_past, n - 1)
                for j in range(NBLK):
                    for xx, parts in ((x3h, (0, 1)), (x3l, (0,))):
                        w = xx[:, h, j, :]
                        for part in parts:
                            first = j == 0 and xx is x3h and part == 0
                            last = xx is x3l
                            if j < 4:
                                nc.tensor.matmul(ps[:, b0, j * P:512], w, g3[:, h, part, 0:512 - j * P],
                                                 start=first, stop=(j == 3 and last))
                            c0 = max(0, 512 - j * P)
                            mm = nc.tensor.matmul(ps[:, b0 + 1, max(0, j * P - 512):512], w, g3[:, h, part, c0:T - j * P],
                                                  start=first, stop=(j == NBLK - 1 and last))
                        mm = nc.tensor.matmul(ps[:, t0 + j // 4, (j % 4) * P:(j % 4 + 1) * P], w, flip[:, :],
                                              start=(xx is x3h), stop=(xx is x3l))
                mm.then_inc(c3_summed, 1)

            def conv1_sums_read(g, h):
                if isinstance(g, int) and g == NG - 1:
                    return HG * NG
                return HG * (g + 1) + 3 + h

            for h in range(HG):
                conv1(0, h)

            def body(g, more1):
                stage2(g)
                if more1:
                    for h in range(HG):
                        conv1(g + 1, h)
                for h in range(HG):
                    conv3(g, h)

            body(0, True)
            with pe.Fori(1, NG - 2) as g:
                body(g, True)
            body(NG - 2, True)
            body(NG - 1, False)

        @block.scalar
        def _(act):
            act.wait_ge(angles_ready, 1)
            nc.scalar.activation(prm[:, 640:832], prm[:, 640:832], ACT.Sin).then_inc(sines_ready, 1)
            nc.scalar.activation(prm[:, 832:896], prm[:, 512:576], ACT.Tanh, scale=0.5).then_inc(sines_ready, 1)
            act.wait_ge(params_turned, 1)
            nc.scalar.activation(tabs[9][:, T:T + 512], ps[:, 0, :], ACT.Copy).then_inc(turned_copied, 1)
            for v in range(2):
                act.wait_ge(angles_ready, v + 2)
                for n in (0, 1, 2):
                    nc.scalar.activation(tabs[n], tabs[n], ACT.Sin)
                for n in (3, 4):
                    e = nc.scalar.activation(tabs[n], tabs[n], ACT.Exp)
                e.then_inc(sines_ready, 1)
                act.wait_ge(k_summed, v + 1)
                act.wait_ge(krow_stored, 16)
                nc.scalar.activation(tabs[7][0:TB, :].rearrange("p (n c) -> p n c", n=4), ps[0:TB, 1:5, :], ACT.Copy,
                                     scale=WS).then_inc(k_scaled, 1)
            act.wait_ge(w0_loaded, 16)
            nc.scalar.activation(w0s[0:NID, :], w0n[0:NID, :], ACT.Copy, scale=WS).then_inc(act_step, 1)
            act.wait_ge(pick_cleared, 1)
            for dgroup in range(8):
                act.wait_ge(pick_summed, 2 * dgroup + 1)
                for q in range(2):
                    rows = slice(q * C, (q + 1) * C)
                    e = nc.scalar.activation(pick[rows, :, 0, q * C + 8 * dgroup:q * C + 8 * dgroup + 8],
                                             ps[rows, 2 * dgroup % 8, :].rearrange("p (e n) -> p n e", e=8), ACT.Copy)
                e.then_inc(pick_hi_copied, 1)

            def split_hi(i, m):
                n = 2 * STEPS * i + m
                act.wait_ge(x_loaded[m % 4], 4 * 16 * i + 16 * (m // 4 + 1))
                at_least(act, s0_summed, n - 1)
                nc.scalar.activation(xh[:, m % 2, :, ::-1], xin[:, m % 4], ACT.Copy, scale=XS).then_inc(x_hi, 1)

            def copy_left(i, m):
                k, g = m // STEPS, m % STEPS
                if g == 0:
                    at_least(act, x1_stored[k], 16 * i)
                act.wait_ge(s0_summed, 2 * STEPS * i + m + 1)
                nc.scalar.activation(xq[:, k, :, 16 * g:16 * g + 8], ps[:, 2 * (m % 4), :].rearrange("p (b d) -> p d b", d=C),
                                     ACT.Copy).then_inc(s0_left_out, 1)

            def stage0(i):
                for m in range(2 * STEPS):
                    split_hi(i, m)
                    if m:
                        copy_left(i, m - 1)
                copy_left(i, 2 * STEPS - 1)

            stage0(0)
            with act.Fori(1, NBLK // 2) as i:
                stage0(i)

            for n in range(NTURN):
                act.wait_ge(w2_turned, n + 1)
                nc.scalar.activation(turned_target(n, 0), ps[:, n % 4, :].rearrange("p (m o) -> p m o", m=4), ACT.Copy,
                                     scale=WS).then_inc(w2_hi, 1)

            def x1_split_hi(g, h):
                act.wait_ge(x1_loaded[h], 16 * (g + 1))
                nc.scalar.activation(x1h[:, h], x1f[:, h], ACT.Copy, scale=XS / FS).then_inc(x1_hi, 1)

            def x2_split_hi(g, h):
                act.wait_ge(c1_out, HG * g + h + 1)
                nc.scalar.activation(x2h[:, h], x1f[:, h], ACT.Copy, scale=XS / FS).then_inc(x2_hi, 1)

            for h in range(HG):
                x1_split_hi(0, h)
            for h in range(HG):
                x2_split_hi(0, h)
            for h in range(HG):
                x1_split_hi(1, h)

            def body(g, more1, more2):
                act.wait_ge(low_scaled, g + 1)
                nc.scalar.activation(lowh.rearrange("p (h b) -> p h b", h=HG), lowf, ACT.Copy).then_inc(low_hi, 1)
                for o in range(NBLK):
                    act.wait_ge(s2_summed, NBLK * g + o + 1)
                    nc.scalar.activation(x3h[:, :, o, :], ps[:, 4 + o % 3, :].rearrange("p (h b) -> p h b", h=HG), ACT.Identity,
                                         bias=biasx[:, o:o + 1], scale=XS / FS).then_inc(x3_hi, 1)
                if more1:
                    for h in range(HG):
                        x2_split_hi(g + 1, h)
                for h in range(HG):
                    act.wait_ge(c3_summed, HG * g + h + 1)
                    at_least(act, out_stored[h], 16 * g)
                    nc.scalar.activation(outt[:, h].rearrange("p (n c) -> p n c", n=2), ps[:, 2 * (h % 2):2 * (h % 2) + 2, :],
                                         ACT.Copy, scale=1.0 / FS).then_inc(c3_out, 1)
                    if more2:
                        x1_split_hi(g + 2, h)

            body(0, True, True)
            with act.Fori(1, NG - 2) as g:
                body(g, True, True)
            body(NG - 2, True, False)
            body(NG - 1, False, False)

        @block.vector
        def _(dve):
            step = [0]

            def link(ins):
                step[0] += 1
                ins.then_inc(dve_step, 1)
                dve.wait_ge(dve_step, step[0])

            ts, tt, stt = nc.vector.tensor_scalar, nc.vector.tensor_tensor, nc.vector.scalar_tensor_tensor

            dve.wait_ge(iota_done, 3)
            dve.wait_ge(ids_loaded, 64)
            nc.vector.tensor_copy(tcol, tcoli)
            nc.vector.tensor_copy(trow[:, 0:T], trowi[:, 0:T])
            nc.vector.tensor_copy(len3f, len3i)
            nc.vector.tensor_copy(idf[:, :, :], ids[:, :, :])
            link(nc.vector.tensor_copy(pcol, pcoli))
            ts(onehot[:, :], idf[0:NID, 0, :], pcol[0:NID, :], None, ALU.is_equal)
            for k in range(NBLK):
                ts(mask1[:, k, :], idf[:, 1, :], tcol[:, k:k + 1], None, ALU.is_gt).then_inc(masks_ready, 1)
            ts(past3[:, :], trow[:, 0:T], len3f, None, ALU.is_ge).then_inc(masks_ready, 1)
            link(ts(rank_adapter, pcol, 1.0 / RANK, -0.5 + 0.5 / RANK, ALU.mult, ALU.add))
            link(ts(rank_adapter, rank_adapter, ROUND, ROUND, ALU.add, ALU.subtract))
            dve.wait_ge(consts_loaded, 16 * (NADAPT + 1))
            link(ts(rank_scale, rank_scale, XS / FS, None, ALU.mult))
            ts(adapter_scale[:, :], idf[:, 2, :], rank_adapter, rank_scale, ALU.is_equal, ALU.mult)
            nc.vector.tensor_copy(bias_rev[0:NBLK, ::-1], biasn[0:NBLK, :])
            link(ts(turn_own, pcol, float(C), 0.25, ALU.is_lt, ALU.mult))
            ts(turn_oth, turn_own, -1.0, 0.25, ALU.mult, ALU.add)
            link(ts(phase_own, turn_own, 2 * math.pi, None, ALU.mult))
            link(ts(phase_oth, phase_own, -1.0, math.pi / 2, ALU.mult, ALU.add))

            def col(n, w=64):
                return prm[:, 64 * n:64 * n + w]

            dve.wait_ge(ssm_loaded, 160)

            def exp_exact(dst, src, w, t1, t2, t3):
                link(ts(t1, src, 1.0 / math.log(2.0), ROUND, ALU.mult, ALU.add))
                link(ts(t1, t1, ROUND, None, ALU.subtract))
                link(stt(t2, t1, -LN2_HI, src, ALU.mult, ALU.add))
                link(stt(t2, t1, -LN2_LO, t2, ALU.mult, ALU.add))
                link(ts(t3, t2, 1.0 / 5040, None, ALU.mult))
                for c in (720, 120, 24, 6, 2, 1):
                    link(stt(t3, t3, 1.0 / c, t2, ALU.add, ALU.mult))
                link(ts(t3, t3, 1.0, None, ALU.add))
                link(ts(t1.bitcast(I32), t1, 127.0, 8388608.0, ALU.add, ALU.mult))
                link(tt(dst, t3, t1, ALU.mult))

            def turns(dst, src, tmp, quarter, phase):
                link(ts(tmp, src, 1.0 / (2 * math.pi), quarter, ALU.mult, ALU.add))
                link(ts(tmp, tmp, ROUND, ROUND, ALU.add, ALU.subtract))
                link(stt(dst, tmp, -TWO_PI_HI, src, ALU.mult, ALU.add))
                link(stt(dst, tmp, -TWO_PI_LO, dst, ALU.mult, ALU.add))
                link(ts(dst, dst, phase, PI_CLAMP, ALU.add, ALU.min))
                link(ts(dst, dst, -PI_CLAMP, None, ALU.max))

            exp_exact(prm[:, 448:449], prm[:, 0:1], 1, prm[:, 449:450], prm[:, 450:451], prm[:, 451:452])
            dt = prm[:, 448:449]
            t = [col(n) for n in range(16, 32)]
            exp_exact(t[0], col(1), 64, t[1], t[2], t[3])
            ar, ai = t[0], col(2)
            re, im = col(8), col(9)
            link(ts(re, ar, dt, -1.0, ALU.mult, ALU.mult))
            link(ts(im, ai, dt, None, ALU.mult))
            link(ts(ar, ar, -1.0, None, ALU.mult))
            link(ts(t[4], im, 0.5, None, ALU.mult))
            turns(col(10), im, t[5], 0.0, 0.0)
            turns(col(11), im, t[5], 0.25, math.pi / 2)
            turns(col(12), t[4], t[5], 0.0, 0.0)
            exp_exact(t[6], re, 64, t[1], t[2], t[3])
            tt(t[5], ar, ar, ALU.mult).then_inc(angles_ready, 1)
            link(tt(t[4], ai, ai, ALU.mult))
            link(tt(t[4], t[4], t[5], ALU.add))
            link(nc.vector.reciprocal(t[7], t[4]))
            dve.wait_ge(sines_ready, 2)
            sin, cos, sinh2, tanh = col(10), col(11), col(12), col(13)
            link(ts(t[1], t[6], 1.0, None, ALU.add))
            link(tt(t[1], t[1], tanh, ALU.mult))
            link(tt(t[1], t[1], cos, ALU.mult))
            link(tt(t[2], sinh2, sinh2, ALU.mult))
            link(stt(t[1], t[2], -2.0, t[1], ALU.mult, ALU.add))
            link(tt(t[2], t[6], sin, ALU.mult))
            cr = prm[:, 192:320].rearrange("p (n r) -> p r n", r=2)[:, 0, :]
            ci = prm[:, 192:320].rearrange("p (n r) -> p r n", r=2)[:, 1, :]

            def complex_mult(o_re, o_im, a_re, a_im, b_re, b_im, t1):
                link(tt(o_re, a_re, b_re, ALU.mult))
                link(tt(t1, a_im, b_im, ALU.mult))
                link(tt(o_re, o_re, t1, ALU.subtract))
                link(tt(o_im, a_re, b_im, ALU.mult))
                link(tt(t1, a_im, b_re, ALU.mult))
                link(tt(o_im, o_im, t1, ALU.add))

            complex_mult(t[8], t[9], cr, ci, t[1], t[2], t[3])
            link(ts(t[10], ai, -1.0, None, ALU.mult))
            complex_mult(t[11], t[12], t[8], t[9], ar, t[10], t[3])
            link(tt(t[11], t[11], t[7], ALU.mult))
            link(tt(t[12], t[12], t[7], ALU.mult))
            big = prm[:, 1024:1536]
            nc.vector.tensor_copy(big[:, 0:64], re)
            nc.vector.tensor_copy(big[:, 64:128], re)
            nc.vector.tensor_copy(big[:, 128:192], im)
            nc.vector.tensor_copy(big[:, 192:256], im)
            ts(big[:, 256:320], t[11], 2.0, None, ALU.mult)
            ts(big[:, 320:384], t[11], -2.0, None, ALU.mult)
            ts(big[:, 384:448], t[12], -2.0, None, ALU.mult)
            ts(big[:, 448:512], t[12], -2.0, None, ALU.mult)
            ts(d_row[0:1, :], prm[0:1, 320:448], 1.0, WS, ALU.add, ALU.mult).then_inc(params_ready, 1)

            right_l = trow[:, 0:TB].rearrange("p (o l) -> p o l", o=1).to_broadcast([P, C, TB])
            left_l = trow[:, 0:TB * TB].rearrange("p (o l s) -> p o l s", o=1, s=TB)[:, :, :, 0].to_broadcast([P, C, TB])
            dve.wait_ge(params_turned, 1)
            ts(biasx[:, :], ps[:, 1, 0:NBLK], XS, None, ALU.mult)
            dve.wait_ge(turned_copied, 1)

            def wide(n):
                return tabs[n].rearrange("p (h l) -> p h l", h=C)

            for v in range(2):
                def turned(n):
                    c = T + n * P + v * C
                    return trow[:, c:c + C].rearrange("p (h o) -> p h o", o=1).to_broadcast([P, C, TB])

                if v:
                    dve.wait_ge(k_summed, 1)
                link(tt(wide(3), turned(1), right_l, ALU.mult))
                turns(tabs[0], tabs[3], tabs[4], turn_own, phase_own)
                link(tt(wide(3), turned(1), left_l, ALU.mult))
                turns(tabs[1], tabs[3], tabs[4], turn_own, phase_own)
                turns(tabs[2], tabs[3], tabs[4], turn_oth, phase_oth)
                tt(wide(3), turned(0), right_l, ALU.mult)
                tt(wide(4), turned(0), left_l, ALU.mult).then_inc(angles_ready, 1)
                dve.wait_ge(sines_ready, 3 + v)
                if v:
                    dve.wait_ge(krow_stored, 48)
                link(tt(tabs[5], tabs[0], tabs[3], ALU.mult))
                link(tt(wide(1), wide(1), turned(2), ALU.mult))
                link(tt(wide(2), wide(2), turned(3), ALU.mult))
                link(tt(tabs[1], tabs[1], tabs[2], ALU.add))
                tt(tabs[6], tabs[1], tabs[4], ALU.mult).then_inc(tables_ready, 1)
                dve.wait_ge(k_scaled, v + 1)
                k0 = tabs[7][0:1, :].rearrange("p (h l) -> p h l", h=C)[:, :, 0]
                link(tt(k0, k0, d_row[0:1, v * C:(v + 1) * C], ALU.add))
                hi = tabs[5][0:TB, v * 1024:(v + 1) * 1024].bitcast(F16)
                lo = tabs[6][0:TB, v * 1024:(v + 1) * 1024].bitcast(F16)
                nc.vector.tensor_copy(hi, tabs[7][0:TB, :]).then_inc(k_split, 1)
                dve.wait_ge(k_split, 2 * v + 1)
                tt(lo, tabs[7][0:TB, :], hi, ALU.subtract).then_inc(k_split, 1)

            dve.wait_ge(act_step, 1)
            diag = w0s[0:NID, 0:C * C]
            diag = bass.AP(diag.tensor, diag.offset, [diag.ap[0], [C + 1, C]])
            link(ts(diag, diag, WS, None, ALU.add))
            link(nc.vector.tensor_copy(w0h[0:NID, :], w0s[0:NID, :]))
            tt(w0l[0:NID, :], w0s[0:NID, :], w0h[0:NID, :], ALU.subtract).then_inc(w0_split, 2)
            dve.wait_ge(pick_cleared, 1)
            for dgroup in range(8):
                dve.wait_ge(pick_summed, 2 * dgroup + 2)
                for q in range(2):
                    rows = slice(q * C, (q + 1) * C)
                    e = nc.vector.tensor_copy(pick[rows, :, 1, q * C + 8 * dgroup:q * C + 8 * dgroup + 8],
                                              ps[rows, (2 * dgroup + 1) % 8, :].rearrange("p (e n) -> p n e", e=8))
                e.then_inc(pick_lo_copied, 1)

            def split_lo(i, m):
                dve.wait_ge(x_hi, 2 * STEPS * i + m + 1)
                stt(xl[:, m % 2, :, ::-1], xin[:, m % 4], XS, xh[:, m % 2, :, ::-1], ALU.mult, ALU.subtract).then_inc(x_lo, 1)

            def copy_right(i, m):
                k, g = m // STEPS, m % STEPS
                if g == 0:
                    at_least(dve, x1_stored[k], 16 * i)
                dve.wait_ge(s0_summed, 2 * STEPS * i + m + 1)
                nc.vector.tensor_copy(xq[:, k, :, 16 * g + 8:16 * g + 16],
                                      ps[:, 2 * (m % 4) + 1, :].rearrange("p (b d) -> p d b", d=C)).then_inc(s0_right_out, 1)

            def stage0(i):
                for m in range(2 * STEPS):
                    split_lo(i, m)
                    if m:
                        copy_right(i, m - 1)
                copy_right(i, 2 * STEPS - 1)

            stage0(0)
            with dve.Fori(1, NBLK // 2) as i:
                stage0(i)

            dve.wait_ge(w2_loaded, 16 * (2 + NADAPT))
            for k in range(NBLK):
                e = nc.vector.tensor_copy(w2r[:, k].rearrange("p (m i) -> p m i", m=NBLK)[:, :, ::-1],
                                          w2n[:, k].rearrange("p (m i) -> p m i", m=NBLK))
            link(e)
            for k in range(NBLK):
                own = w2r[:, k, k * P:(k + 1) * P]
                stt(own, flip[:, :], XS, own, ALU.mult, ALU.add)
            nc.vector.tensor_copy(a_rev.rearrange("p (m i) -> p m i", m=NBLK)[:, :, ::-1],
                                  an.rearrange("p (m i) -> p m i", m=NBLK)).then_inc(w2_ready, 1)
            for n in range(NTURN):
                dve.wait_ge(w2_hi, n + 1)
                stt(turned_target(n, 1), ps[:, n % 4, :].rearrange("p (m o) -> p m o", m=4), WS, turned_target(n, 0),
                    ALU.mult, ALU.subtract).then_inc(w2_lo, 1)

            def turn_g1(g, h):
                dve.wait_ge(g1_loaded[h], 16 * (g + 1))
                at_least(dve, c1_summed, HG * (g - 1) + h + 1)
                nc.vector.tensor_copy(g1[:, h].rearrange("p s (d t) -> p (s d) t", t=P)[:, :, ::-1],
                                      g1n[:, h % 2].rearrange("p s (d t) -> p (s d) t", t=P)).then_inc(g1_turned, 1)

            gate = small[:, 40:40 + 2 * HG]
            dve.wait_ge(masks_ready, NBLK + 1)
            def x1_split_lo(g, h):
                dve.wait_ge(x1_hi, HG * g + h + 1)
                stt(x1l[:, h], x1f[:, h], XS / FS, x1h[:, h], ALU.mult, ALU.subtract).then_inc(x1_lo, 1)

            def take_conv1(g, h):
                dve.wait_ge(c1_summed, HG * g + h + 1)
                nc.vector.memset(gate[:, h:h + 1], 0.0)
                b0 = 2 * (h % 2)
                nc.vector.copy_predicated(x1f[:, h].rearrange("p k b -> p (k b)"), mask1[:, :, :].rearrange("p k b -> p (k b)"),
                                          ps[:, b0:b0 + 2, :].rearrange("p n c -> p (n c)")).then_inc(c1_out, 1)

            def x2_split_lo(g, h):
                dve.wait_ge(x2_hi, HG * g + h + 1)
                stt(x2l[:, h], x1f[:, h], XS / FS, x2h[:, h], ALU.mult, ALU.subtract).then_inc(x2_lo, 1)

            def conv1(g):
                for h in range(HG):
                    take_conv1(g, h)
                    if h:
                        x2_split_lo(g, h - 1)
                x2_split_lo(g, HG - 1)

            for h in range(HG):
                turn_g1(0, h)
            for h in range(HG):
                x1_split_lo(0, h)
            conv1(0)
            for h in range(HG):
                turn_g1(1, h)
                x1_split_lo(1, h)

            def body(g, more1, more2):
                dve.wait_ge(low_summed, g + 1)
                tt(lowf, ps[:, 7, :].rearrange("p (h b) -> p h b", h=HG),
                   adapter_scale[:, :].rearrange("p (o b) -> p o b", o=1).to_broadcast([P, HG, B]), ALU.mult).then_inc(low_scaled, 1)
                dve.wait_ge(low_hi, g + 1)
                tt(lowl.rearrange("p (h b) -> p h b", h=HG), lowf, lowh.rearrange("p (h b) -> p h b", h=HG),
                   ALU.subtract).then_inc(low_lo, 1)

                def lo3(o):
                    dve.wait_ge(s2_out, NBLK * g + o + 1)
                    tt(x3l[:, :, o, :], x3f[:, o % 2], x3h[:, :, o, :], ALU.subtract).then_inc(x3_lo, 1)

                for o in range(NBLK):
                    if o >= 2:
                        dve.wait_ge(x3_lo, NBLK * g + o - 1)
                    dve.wait_ge(x3_hi, NBLK * g + o + 1)
                    ts(x3f[:, o % 2], ps[:, 4 + o % 3, :].rearrange("p (h b) -> p h b", h=HG), XS / FS, biasx[:, o:o + 1],
                       ALU.mult, ALU.add).then_inc(s2_out, 1)
                    if o:
                        lo3(o - 1)
                lo3(NBLK - 1)
                if more1:
                    conv1(g + 1)
                for h in range(HG):
                    dve.wait_ge(c3_out, HG * g + h + 1)
                    nc.vector.memset(gate[:, HG + h:HG + h + 1], 0.0)
                    t0 = 4 + 2 * (h % 2)
                    nc.vector.copy_predicated(outt[:, h], past3[:, :],
                                              ps[:, t0:t0 + 2, :].rearrange("p n c -> p (n c)")).then_inc(c3_past, 1)
                    if more2:
                        turn_g1(g + 2, h)
                        x1_split_lo(g + 2, h)

            body(0, True, True)
            with dve.Fori(1, NG - 2) as g:
                body(g, True, True)
            body(NG - 2, True, False)
            body(NG - 1, False, False)


_INS = ['x', 'itok_B_0_15', 'itok_B_78_3631', 'itok_B_1_7', 'itok_B_8_3872', 'L0_cond_weights',
        'L1_cond_log_dt', 'L1_cond_C', 'L1_cond_log_A_real', 'L1_cond_A_imag', 'L1_cond_D',
        'L2_cond_weight', 'L2_cond_bias', 'L2_cond_lora_a_weights', 'L2_cond_lora_b_weights', 'L2_cond_scaling_factors',
        'L3_cond_log_dt', 'L3_cond_C', 'L3_cond_log_A_real', 'L3_cond_A_imag', 'L3_cond_D']


def kernel(**inputs):
    import numpy as _np
    import concourse.bacc as _bacc
    from concourse import mybir as _mybir
    from concourse.bass_utils import run_bass_kernel_spmd as _run

    nc = _bacc.Bacc("TRN2", target_bir_lowering=False, num_devices=1)
    arrays, ap = {}, {}
    for name in _INS:
        a = _np.ascontiguousarray(inputs[name])
        arrays[f"in_{name}_dram"] = a
        ap[name] = nc.dram_tensor(f"in_{name}_dram", a.shape, _mybir.dt.from_np(a.dtype), kind="ExternalInput").ap()
    out = nc.dram_tensor("out_0_dram", (B, C, T), _mybir.dt.float32, kind="ExternalOutput").ap()

    def ssm(p):
        return tuple(ap[f"{p}_cond_{n}"] for n in ("log_dt", "C", "log_A_real", "A_imag", "D"))

    build(nc, ap['x'], ap['itok_B_0_15'], ap['itok_B_78_3631'], ap['itok_B_1_7'], ap['itok_B_8_3872'],
          ap['L0_cond_weights'], ssm("L1"), ssm("L3"), ap['L2_cond_weight'], ap['L2_cond_bias'],
          ap['L2_cond_lora_a_weights'], ap['L2_cond_lora_b_weights'], ap['L2_cond_scaling_factors'], out)
    r = _run(nc, [arrays], core_ids=[0])
    return r.results[0]["out_0_dram"]
```

```python
import math
from contextlib import ExitStack

import concourse.bass as bass
from concourse import mybir

ALU = mybir.AluOpType
ACT = mybir.ActivationFunctionType
F32 = mybir.dt.float32
F16 = mybir.dt.float16
I32 = mybir.dt.int32
U8 = mybir.dt.uint8

P = 128
B, C, T = 128, 64, 1024
NBLK = T // P
NID, NADAPT, RANK = 16, 8, 16
NMODE = 64
XS, WS = 32.0, 64.0
FS = XS * WS
PAIRS = B // 2
NXIN = 4
GPAIRS = 8
STEPS = PAIRS // GPAIRS
NPART = 4
HG = 4
NG = C // HG
COLS = HG * B
TB = 32
CH = 2 * C // NBLK
KROW = P + T

ROUND = 12582912.0
TWO_PI_HI = 6.28125
TWO_PI_LO = 2 * math.pi - TWO_PI_HI
LN2_HI = 0.693359375
LN2_LO = math.log(2.0) - LN2_HI
PI_CLAMP = 3.1415925
TURN = 6.2831845


def at_least(engine, semaphore, value):
    if not (isinstance(value, int) and value <= 0):
        engine.wait_ge(semaphore, value)


def build(nc, x, ids0, len1, ids2, len3, w0, ssm1, ssm3, w2, bias2, lora_a, lora_b, lora_s, out):
    with ExitStack() as ctx:
        def sem(name):
            return ctx.enter_context(nc.semaphore(name))

        def sb(name, shape, dt):
            return ctx.enter_context(nc.sbuf_tensor(name, shape, dt))

        x1_dram = nc.dram_tensor("x1_scratch", [NBLK, P, C, B], F32).ap()
        krow_t = nc.dram_tensor("krow_scratch", [2, C, 2, KROW], F16)
        krow = krow_t.ap()

        ps = ctx.enter_context(nc.psum_tensor("ps", [P, 8, 512], F32))

        ident = sb("ident", [P, P], F32)
        w2t = sb("w2t", [P, 2, NBLK, T], F16)
        at = sb("at", [P, 2, NBLK, P], F16)
        bt = sb("bt", [P, 2, T], F16)
        adapter_scale = sb("adapter_scale", [P, B], F32)
        biasx = sb("biasx", [P, NBLK], F32)
        mask1 = sb("mask1", [P, NBLK, B], U8)
        past3 = sb("past3", [P, T], U8)
        flip = sb("flip", [P, P], F16)
        gbuf = sb("gbuf", [P, 40 * 256], F32)

        def part_of(tile, at_kb, kb, dt=F32):
            v = tile[:, int(at_kb * 256):int((at_kb + kb) * 256)]
            return v if dt == F32 else v.bitcast(dt)

        g1 = part_of(gbuf, 0, 16, F16).rearrange("p (h s t) -> p h s t", h=HG, s=2)
        g3 = part_of(gbuf, 16, 16, F16).rearrange("p (h s t) -> p h s t", h=HG, s=2)
        g1n = part_of(gbuf, 32, 8, F16).rearrange("p (h s t) -> p h s t", h=2, s=2)
        prm = part_of(gbuf, 0, 8)
        turned = part_of(gbuf, 8, 2).rearrange("p (n r) -> p n r", n=4)
        trow = part_of(gbuf, 10, 4)
        trowi = part_of(gbuf, 14, 4, I32)
        kf = part_of(gbuf, 14, 2)
        kh = part_of(gbuf, 16, 1, F16)
        kl = part_of(gbuf, 17, 1, F16)
        biasn = part_of(gbuf, 18, 0.5)
        bias_rev = part_of(gbuf, 18.5, 0.5)
        angle_r, angle_l, turn_r, turn_own, turn_oth = [part_of(gbuf, 19 + 2 * n, 2) for n in range(5)]
        wrow = part_of(gbuf, 29, 4)
        wrow_rev = part_of(gbuf, 33, 4)
        ids = part_of(gbuf, 37, 1.5, I32).rearrange("p (n b) -> p n b", n=3)
        idf = part_of(gbuf, 38.5, 1.5).rearrange("p (n b) -> p n b", n=3)
        small = sb("small", [P, 64], F32)
        d_row = sb("d_row", [1, 2 * C], F32)

        arena = sb("arena", [P, 120 * 256], F32)

        def area(at_kb, kb, dt=F32):
            return part_of(arena, at_kb, kb, dt)

        pick = area(0, 32, F16).rearrange("p (n s d) -> p n s d", n=PAIRS, s=2)
        xin = area(32, 16).rearrange("p (s n t) -> p s n t", s=NXIN, n=GPAIRS)
        xh = area(48, 4, F16).rearrange("p (s n t) -> p s n t", s=2, n=GPAIRS)
        xl = area(52, 4, F16).rearrange("p (s n t) -> p s n t", s=2, n=GPAIRS)
        xq = area(56, 64).rearrange("p (k d b) -> p k d b", k=2, d=C)
        w0n = area(56, 16)
        w0h = area(72, 8, F16)
        w0l = area(80, 8, F16)
        x1f = area(0, 16).rearrange("p (h k b) -> p h k b", h=HG, k=NBLK)
        x1h = area(16, 8, F16).rearrange("p (h k b) -> p h k b", h=HG, k=NBLK)
        x1l = area(24, 8, F16).rearrange("p (h k b) -> p h k b", h=HG, k=NBLK)
        x2h = area(32, 8, F16).rearrange("p (h k b) -> p h k b", h=HG, k=NBLK)
        x2l = area(40, 8, F16).rearrange("p (h k b) -> p h k b", h=HG, k=NBLK)
        x3h = area(48, 8, F16).rearrange("p (h k b) -> p h k b", h=HG, k=NBLK)
        x3l = area(56, 8, F16).rearrange("p (h k b) -> p h k b", h=HG, k=NBLK)
        outt = area(64, 16).rearrange("p (h t) -> p h t", h=HG)
        x3f = area(80, 4).rearrange("p (s h b) -> p s h b", s=2, h=HG)
        lowf = area(84, 2).rearrange("p (h b) -> p h b", h=HG)
        lowh = area(86, 1, F16)
        lowl = area(87, 1, F16)

        half_own = small[:, 10:12]
        half_oth = small[:, 12:14]
        act_gate = small[:, 48:49]
        pcol = small[:, 0:1]
        phase_own = small[:, 1:2]
        phase_oth = small[:, 2:3]
        quarter_own = small[:, 3:4]
        quarter_oth = small[:, 4:5]
        rank_scale = small[:, 5:6]
        rank_adapter = small[:, 6:7]
        len3f = small[:, 7:8]
        len3i = small[:, 8:9].bitcast(I32)
        pcoli = small[:, 9:10].bitcast(I32)
        tcol = small[:, 16:24]
        tcoli = small[:, 24:32].bitcast(I32)
        onehot = sb("onehot", [NID, B], F16)
        zrow = sb("zrow", [P, P], F32)

        consts_loaded = sem("consts_loaded")
        iota_done = sem("iota_done")
        ids_loaded = sem("ids_loaded")
        w0_loaded = sem("w0_loaded")
        ssm_loaded = sem("ssm_loaded")
        dve_step = sem("dve_step")
        table_step = sem("table_step")
        masks_ready = sem("masks_ready")
        params_ready = sem("params_ready")
        params_turned = sem("params_turned")
        turned_copied = sem("turned_copied")
        angles_ready = sem("angles_ready")
        sines_ready = sem("sines_ready")
        table_angles = sem("table_angles")
        table_sines = sem("table_sines")
        tables_ready = sem("tables_ready")
        k_summed = sem("k_summed")
        k_scaled = sem("k_scaled")
        k_hi = sem("k_hi")
        k_split = sem("k_split")
        krow_stored = sem("krow_stored")
        zeros_ready = sem("zeros_ready")
        w0_ready = sem("w0_ready")
        w0_hi = sem("w0_hi")
        w0_lo = sem("w0_lo")
        pick_cleared = sem("pick_cleared")
        pick_summed = sem("pick_summed")
        pick_hi_copied = sem("pick_hi_copied")
        pick_lo_copied = sem("pick_lo_copied")
        x_loaded = [sem(f"x_loaded{s}") for s in range(4)]
        x_hi = sem("x_hi")
        x_lo = sem("x_lo")
        s0_summed = sem("s0_summed")
        s0_left_out = sem("s0_left_out")
        s0_right_out = sem("s0_right_out")
        x1_stored = [[sem(f"x1_stored{k}{part}") for part in range(NPART)] for k in range(2)]
        wrow_loaded = sem("wrow_loaded")
        w2_rev = sem("w2_rev")
        w2_ready = sem("w2_ready")
        w2_turned = sem("w2_turned")
        w2_hi = sem("w2_hi")
        w2_lo = sem("w2_lo")
        x1_loaded = [sem(f"x1_loaded{h}") for h in range(HG)]
        g1_loaded = [sem(f"g1_loaded{h}") for h in range(HG)]
        g3_loaded = [sem(f"g3_loaded{h}") for h in range(HG)]
        out_stored = [sem(f"out_stored{h}") for h in range(HG)]
        x1_hi = sem("x1_hi")
        x1_lo = sem("x1_lo")
        g1_turned = sem("g1_turned")
        c1_summed = sem("c1_summed")
        c1_out = sem("c1_out")
        x2_hi = sem("x2_hi")
        x2_lo = sem("x2_lo")
        low_summed = sem("low_summed")
        low_scaled = sem("low_scaled")
        low_hi = sem("low_hi")
        low_lo = sem("low_lo")
        s2_summed = sem("s2_summed")
        x3_hi = sem("x3_hi")
        s2_out = sem("s2_out")
        x3_lo = sem("x3_lo")
        c3_summed = sem("c3_summed")
        c3_out = sem("c3_out")
        c3_past = sem("c3_past")

        ssm = (ssm1, ssm3)
        LOT_B, LOT_A, LOT_W = 0, 1, 2

        x_pairs = x.rearrange("(n q) c t -> (q c) n t", q=2)

        def lot_target(n, part):
            if isinstance(n, int) and n == LOT_B:
                return bt[:, part, :].rearrange("p (m o) -> p m o", m=NBLK)
            if isinstance(n, int) and n == LOT_A:
                return at[:, part, :, :]
            return w2t[:, part, :, bass.ds((n - LOT_W) * P, P)]

        def turned_tiles(n):
            tiles = ps[:, 6:8, :].rearrange("p q (m o) -> p (q m) o", m=4)
            return tiles if isinstance(n, int) and n == LOT_A else tiles[:, :, ::-1]

        def wide(tile):
            return tile.rearrange("p (h l) -> p h l", h=CH)

        block = ctx.enter_context(nc.Block())

        @block.sync
        def _(sp):
            sp.dma_start(w0n[0:NID, :], w0.rearrange("i c d -> i (c d)")).then_inc(w0_loaded, 16)
            for n, row in enumerate((ids0, len1, ids2)):
                sp.dma_start(ids[:, n, :], row.rearrange("(o b) -> o b", o=1).to_broadcast([P, B])).then_inc(ids_loaded, 16)
            sp.dma_start(len3i, len3.rearrange("(b o) -> b o", o=1)).then_inc(ids_loaded, 16)

            def load_x(i, m):
                k, g = m // STEPS, m % STEPS
                n = 2 * STEPS * i + m
                at_least(sp, x_hi, n - 3)
                at_least(sp, x_lo, n - 3)
                t0 = (2 * i + k) * P
                sp.dma_start(xin[:, m % 4], x_pairs[:, g * GPAIRS:(g + 1) * GPAIRS, bass.ds(t0, P)]).then_inc(x_loaded[m % 4], 16)

            def store_x1(i, k):
                sp.wait_ge(s0_left_out, (2 * i + k + 1) * STEPS)
                sp.wait_ge(s0_right_out, (2 * i + k + 1) * STEPS)
                for part in range(NPART):
                    d0 = part * (C // NPART)
                    sp.dma_start(x1_dram[bass.ds(2 * i + k, 1), :, d0:d0 + C // NPART, :].rearrange("o p d b -> (o p) (d b)"),
                                 xq[:, k, d0:d0 + C // NPART].rearrange("p d b -> p (d b)")).then_inc(x1_stored[k][part], 16)

            def stage0(i, first):
                for m in range(2 * STEPS):
                    load_x(i, m)
                    if m == 3 and not first:
                        store_x1(i - 1, 1)
                    if m == STEPS + 3:
                        store_x1(i, 0)

            stage0(0, True)
            with sp.Fori(1, NBLK // 2) as i:
                stage0(i, False)
            store_x1(NBLK // 2 - 1, 1)

            def load_g(v, g, h):
                tile = (g1n[:, h % 2], g3[:, h])[v]
                src = bass.AP(krow_t, (HG * g + h) * (2 * KROW) + v * (C * 2 * KROW) + 1, [[1, P], [KROW, 2], [1, T]])
                sp.dma_start(tile, src).then_inc((g1_loaded, g3_loaded)[v][h], 16)

            def load_x1(g, h):
                src = x1_dram.rearrange("k p d b -> p d k b")[:, bass.ds(HG * g + h, 1)].rearrange("p o k b -> p (o k) b")
                sp.dma_start(x1f[:, h], src).then_inc(x1_loaded[h], 16)

            def load_g1(g, h):
                at_least(sp, g1_turned, HG * g + h - 1)
                load_g(0, g, h)

            sp.wait_ge(krow_stored, 16 + 32 * NBLK)
            sp.wait_ge(w2_lo, LOT_W + NBLK)
            for h in range(2):
                load_g1(0, h)
            sp.wait_ge(s0_summed, NBLK * STEPS)
            for part in range(NPART):
                for k in range(2):
                    sp.wait_ge(x1_stored[k][part], 16 * NBLK // 2)
                if part == 0:
                    for h in range(HG):
                        load_x1(0, h)
            for h in range(2, HG):
                load_g1(0, h)
            for h in range(HG):
                load_g(1, 0, h)

            def reload_first(g, h):
                load_g1(g, h)
                sp.wait_ge(x2_hi, HG * (g - 1) + h + 1)
                sp.wait_ge(x2_lo, HG * (g - 1) + h + 1)
                load_x1(g, h)

            for h in range(HG):
                reload_first(1, h)

            def body(g, more1, more2):
                if more2:
                    for h in range(HG):
                        reload_first(g + 2, h)
                for h in range(HG):
                    sp.wait_ge(c3_past, HG * g + h + 1)
                    sp.dma_start(out[:, bass.ds(HG * g + h, 1), :].rearrange("b o t -> b (o t)"), outt[:, h]).then_inc(out_stored[h], 16)
                    if more1:
                        sp.wait_ge(c3_summed, HG * g + h + 1)
                        load_g(1, g + 1, h)

            body(0, True, True)
            with sp.Fori(1, NG - 2) as g:
                body(g, True, True)
            body(NG - 2, True, False)
            body(NG - 1, False, False)
            for h in range(HG):
                sp.wait_ge(out_stored[h], 16 * NG)

        @block.gpsimd
        def _(pool):
            nc.gpsimd.iota(pcoli, [[0, 1]], base=0, channel_multiplier=1).then_inc(iota_done, 1)
            nc.gpsimd.iota(tcoli, [[P, NBLK]], base=P - 1, channel_multiplier=-1).then_inc(iota_done, 1)
            nc.gpsimd.iota(trowi[:, 0:T], [[1, T]], base=0, channel_multiplier=0).then_inc(iota_done, 1)
            nc.gpsimd.memset(ident[:, :], 0.0).then_inc(iota_done, 1)
            nc.gpsimd.memset(flip[:, :], 0.0).then_inc(iota_done, 1)
            pool.wait_ge(iota_done, 5)
            nc.gpsimd.affine_select(out=ident[:, :], in_=ident[:, :], compare_op=ALU.not_equal, fill=1.0, base=0,
                                    pattern=[[-1, P]], channel_multiplier=1).then_inc(iota_done, 1)
            nc.gpsimd.affine_select(out=flip[:, :], in_=flip[:, :], compare_op=ALU.not_equal, fill=1.0 / XS, base=-(P - 1),
                                    pattern=[[1, P]], channel_multiplier=1).then_inc(iota_done, 1)
            nc.gpsimd.memset(zrow[:, :], 0.0).then_inc(zeros_ready, 1)
            nc.gpsimd.memset(area(0, 32), 0.0).then_inc(pick_cleared, 1)

        @block.tensor
        def _(pe):
            pe.wait_ge(w0_hi, 1)
            pe.wait_ge(w0_lo, 1)
            for n in range(16):
                dgroup, part = n // 2, n % 2
                at_least(pe, (pick_hi_copied, pick_lo_copied)[part], dgroup - 3)
                src = (w0h, w0l)[part][0:NID, :].rearrange("i (c d) -> i d c", d=C)
                for e in range(8):
                    for q in range(2):
                        mm = nc.tensor.matmul(ps[q * C:(q + 1) * C, n % 8, e * PAIRS:(e + 1) * PAIRS], src[:, 8 * dgroup + e, :],
                                              onehot[:, :].rearrange("i (n q) -> i q n", q=2)[:, q, :], start=True, stop=True)
                mm.then_inc(pick_summed, 1)
            pe.wait_ge(pick_hi_copied, 8)
            pe.wait_ge(pick_lo_copied, 8)

            def turn_params():
                pe.wait_ge(params_ready, 1)
                nc.tensor.transpose(ps[:, 5, 0:NBLK], bias_rev[0:NBLK, :], ident[0:NBLK, 0:NBLK])
                for n in range(4):
                    mm = nc.tensor.transpose(ps[:, 4, n * P:(n + 1) * P], prm[:, 1024 + n * P:1024 + (n + 1) * P], ident[:, :])
                mm.then_inc(params_turned, 1)

            def sum_k(c):
                pe.wait_ge(tables_ready, c + 1)
                if isinstance(c, int) and c == 0:
                    pe.wait_ge(turned_copied, 1)
                at_least(pe, k_scaled, c)
                for h in range(CH):
                    mm = nc.tensor.matmul(ps[0:TB, 4, h * TB:(h + 1) * TB], turn_own[:, h * TB:(h + 1) * TB],
                                          turn_r[:, h * TB:(h + 1) * TB], start=True, stop=True)
                mm.then_inc(k_summed, 1)

            def turn_lot(n):
                pe.wait_ge(w2_ready, n + 1)
                at_least(pe, w2_hi, n)
                at_least(pe, w2_lo, n)
                for m in range(NBLK):
                    mm = nc.tensor.transpose(ps[:, 6 + m // 4, (m % 4) * P:(m % 4 + 1) * P], wrow_rev[:, m * P:(m + 1) * P],
                                             ident[:, :])
                mm.then_inc(w2_turned, 1)

            def stage0(i, first):
                for m in range(2 * STEPS):
                    n = 2 * STEPS * i + m
                    s = m % 2
                    k, step = m // STEPS, m % STEPS
                    blk = 2 * i + k
                    pe.wait_ge(x_hi, n + 1)
                    pe.wait_ge(x_lo, n + 1)
                    at_least(pe, s0_left_out, n - 1)
                    at_least(pe, s0_right_out, n - 1)
                    for j in range(GPAIRS):
                        o = ps[:, 2 * s + j // 4, (j % 4) * P:(j % 4 + 1) * P]
                        w = pick[:, step * GPAIRS + j]
                        nc.tensor.matmul(o, xh[:, s, j, :], w[:, 0, :], start=True, stop=False)
                        nc.tensor.matmul(o, xh[:, s, j, :], w[:, 1, :], start=False, stop=False)
                        mm = nc.tensor.matmul(o, xl[:, s, j, :], w[:, 0, :], start=False, stop=True)
                    mm.then_inc(s0_summed, 1)
                    if first and k == 0:
                        if step == 1:
                            turn_lot(LOT_B)
                        if step == 4:
                            turn_params()
                            turn_lot(LOT_A)
                        if step == 6:
                            turn_lot(LOT_W)
                        if step == 7:
                            sum_k(0)
                    else:
                        if step == 4:
                            turn_lot(blk + LOT_W)
                        if step == 6:
                            sum_k(blk)

            stage0(0, True)
            with pe.Fori(1, NBLK // 2) as i:
                stage0(i, False)

            pe.wait_ge(s0_left_out, NBLK * STEPS)
            pe.wait_ge(s0_right_out, NBLK * STEPS)
            pe.wait_ge(k_scaled, NBLK)
            pe.wait_ge(w2_hi, LOT_W + NBLK)
            pe.wait_ge(w2_lo, LOT_W + NBLK)

            def conv1(g, h):
                n = HG * g + h
                b0 = 2 * (h % 2)
                pe.wait_ge(g1_turned, n + 1)
                pe.wait_ge(x1_hi, n + 1)
                pe.wait_ge(x1_lo, n + 1)
                if h < 2:
                    at_least(pe, c3_out, HG * (g - 1))
                else:
                    pe.wait_ge(c1_out, n - 1)
                products = [(0, x1h), (0, x1l), (1, x1h)]
                for d in range(NBLK):
                    for q, (part, xx) in enumerate(products):
                        w = g1[:, h, part, d * P:(d + 1) * P]
                        first, last = d == 0 and q == 0, q == 2
                        if d < 4:
                            nc.tensor.matmul(ps[:, b0, d * B:4 * B], w, xx[:, h, 0:4 - d, :],
                                             start=first, stop=(d == 3 and last))
                        lo = max(0, 4 - d)
                        mm = nc.tensor.matmul(ps[:, b0 + 1, (lo + d - 4) * B:4 * B], w, xx[:, h, lo:NBLK - d, :],
                                              start=first, stop=(d == NBLK - 1 and last))
                mm.then_inc(c1_summed, 1)

            def stage2(g):
                pe.wait_ge(x2_hi, HG * (g + 1))
                pe.wait_ge(x2_lo, HG * (g + 1))
                at_least(pe, c3_past, HG * g)
                products = [(0, x2h), (0, x2l), (1, x2h)]
                for k in range(NBLK):
                    for q, (part, xx) in enumerate(products):
                        mm = nc.tensor.matmul(ps[:, 7, :], at[:, part, k, :], xx[:, :, k, :],
                                              start=(k == 0 and q == 0), stop=(k == NBLK - 1 and q == 2))
                mm.then_inc(low_summed, 1)
                for o in range(NBLK):
                    if o >= 3:
                        pe.wait_ge(s2_out, NBLK * g + o - 2)
                    for k in range(NBLK):
                        for q, (part, xx) in enumerate(products):
                            nc.tensor.matmul(ps[:, 4 + o % 3, :], w2t[:, part, k, o * P:(o + 1) * P], xx[:, :, k, :],
                                             start=(k == 0 and q == 0), stop=False)
                    if o == 0:
                        pe.wait_ge(low_hi, g + 1)
                        pe.wait_ge(low_lo, g + 1)
                    for q, (part, xx) in enumerate([(0, lowh), (0, lowl), (1, lowh)]):
                        mm = nc.tensor.matmul(ps[:, 4 + o % 3, :], bt[:, part, o * P:(o + 1) * P], xx, start=False, stop=(q == 2))
                    mm.then_inc(s2_summed, 1)

            def conv3(g, h):
                n = HG * g + h
                b0, t0 = 2 * (h % 2), 4 + 2 * (h % 2)
                pe.wait_ge(g3_loaded[h], 16 * (g + 1))
                if h == 0:
                    pe.wait_ge(x3_hi, NBLK * (g + 1))
                    pe.wait_ge(x3_lo, NBLK * (g + 1))
                if h < 2:
                    pe.wait_ge(c1_out, conv1_sums_read(g, h))
                else:
                    pe.wait_ge(c3_out, n - 1)
                    pe.wait_ge(c3_past, n - 1)
                for j in range(NBLK):
                    for xx, parts in ((x3h, (0, 1)), (x3l, (0,))):
                        w = xx[:, h, j, :]
                        for part in parts:
                            first = j == 0 and xx is x3h and part == 0
                            last = xx is x3l
                            if j < 4:
                                nc.tensor.matmul(ps[:, b0, j * P:512], w, g3[:, h, part, 0:512 - j * P],
                                                 start=first, stop=(j == 3 and last))
                            c0 = max(0, 512 - j * P)
                            mm = nc.tensor.matmul(ps[:, b0 + 1, max(0, j * P - 512):512], w, g3[:, h, part, c0:T - j * P],
                                                  start=first, stop=(j == NBLK - 1 and last))
                        mm = nc.tensor.matmul(ps[:, t0 + j // 4, (j % 4) * P:(j % 4 + 1) * P], w, flip[:, :],
                                              start=(xx is x3h), stop=(xx is x3l))
                mm.then_inc(c3_summed, 1)

            def conv1_sums_read(g, h):
                if isinstance(g, int) and g == NG - 1:
                    return HG * NG
                return HG * (g + 1) + 3 + h

            for h in range(HG):
                conv1(0, h)

            def body(g, more1):
                stage2(g)
                if more1:
                    for h in range(HG):
                        conv1(g + 1, h)
                for h in range(HG):
                    conv3(g, h)

            body(0, True)
            with pe.Fori(1, NG - 2) as g:
                body(g, True)
            body(NG - 2, True)
            body(NG - 1, False)

        @block.scalar
        def _(act):
            def load_lot(n):
                at_least(act, w2_ready, n)
                if isinstance(n, int) and n == LOT_B:
                    for a in range(NADAPT):
                        act.dma_start(wrow.rearrange("p (k a r) -> p k a r", k=NBLK, a=NADAPT)[:, :, a, :],
                                      lora_b[a].rearrange("(k o) r -> o k r", k=NBLK)).then_inc(wrow_loaded, 16)
                elif isinstance(n, int) and n == LOT_A:
                    act.dma_start(wrow, lora_a.rearrange("a r i -> (a r) i")).then_inc(wrow_loaded, 16)
                else:
                    act.dma_start(wrow, w2[bass.ds((n - LOT_W) * P, P), :]).then_inc(wrow_loaded, 16)

            def store_k(c):
                act.wait_ge(k_split, c + 1)
                rows = krow.rearrange("v h s n -> (v h) s n")[bass.ds(c * CH, CH)]
                for part, half in enumerate((kh, kl)):
                    act.dma_start(rows[:, part, P:].rearrange("h (a b) -> a h b", a=TB),
                                  half[0:TB, :].rearrange("a (h b) -> a h b", h=CH)).then_inc(krow_stored, 16)

            for v in range(2):
                rows = slice(v * C, (v + 1) * C)
                log_dt, cc, log_ar, a_imag, dd = ssm[v]
                act.dma_start(prm[rows, 0:1], log_dt.rearrange("(h o) -> h o", o=1)).then_inc(ssm_loaded, 16)
                act.dma_start(prm[rows, 64:128], log_ar).then_inc(ssm_loaded, 16)
                act.dma_start(prm[rows, 128:192], a_imag).then_inc(ssm_loaded, 16)
                act.dma_start(prm[rows, 192:320], cc.rearrange("h n r -> h (n r)")).then_inc(ssm_loaded, 16)
                act.dma_start(prm[0:1, 320 + v * C:320 + (v + 1) * C], dd.rearrange("(o h) -> o h", o=1)).then_inc(ssm_loaded, 16)
            load_lot(LOT_B)
            for a in range(NADAPT):
                act.dma_start(rank_scale[a * RANK:(a + 1) * RANK, :],
                              lora_s[a:a + 1].rearrange("(o a) -> o a", o=1).to_broadcast([RANK, 1])).then_inc(consts_loaded, 16)
            act.dma_start(biasn[0:NBLK, :], bias2.rearrange("(k o) -> k o", k=NBLK)).then_inc(consts_loaded, 16)
            act.wait_ge(zeros_ready, 1)
            act.dma_start(krow.rearrange("v h s n -> (v h) s n")[:, :, 0:P],
                          zrow[:, :].bitcast(F16).rearrange("p (s n) -> p s n", s=2)).then_inc(krow_stored, 16)

            act.wait_ge(w0_ready, 1)
            nc.scalar.activation(w0h[0:NID, :], w0n[0:NID, :], ACT.Copy, scale=WS).then_inc(w0_hi, 1)
            act.wait_ge(pick_cleared, 1)
            for dgroup in range(8):
                act.wait_ge(pick_summed, 2 * dgroup + 1)
                for q in range(2):
                    rows = slice(q * C, (q + 1) * C)
                    e = nc.scalar.activation(pick[rows, :, 0, q * C + 8 * dgroup:q * C + 8 * dgroup + 8],
                                             ps[rows, 2 * dgroup % 8, :].rearrange("p (e n) -> p n e", e=8), ACT.Copy)
                e.then_inc(pick_hi_copied, 1)

            def param_sines():
                act.wait_ge(angles_ready, 1)
                nc.scalar.activation(prm[:, 640:832], prm[:, 640:832], ACT.Sin).then_inc(sines_ready, 1)
                nc.scalar.activation(prm[:, 832:896], prm[:, 512:576], ACT.Tanh, scale=0.5).then_inc(sines_ready, 1)

            def copy_turned():
                act.wait_ge(params_turned, 1)
                nc.scalar.activation(turned.rearrange("p n r -> p (n r)"), ps[:, 4, :], ACT.Copy).then_inc(turned_copied, 1)

            def chunk_sines(c):
                act.wait_ge(table_angles, c + 1)
                nc.scalar.activation(turn_r, turn_r, ACT.Sin, bias=phase_own, scale=-TURN)
                nc.scalar.activation(turn_own, turn_own, ACT.Sin, bias=phase_own, scale=-TURN)
                nc.scalar.activation(turn_oth, turn_oth, ACT.Sin, bias=phase_oth, scale=-TURN)
                nc.scalar.activation(angle_r, angle_r, ACT.Exp)
                nc.scalar.activation(angle_l, angle_l, ACT.Exp).then_inc(table_sines, 1)

            def scale_k(c):
                act.wait_ge(k_summed, c + 1)
                nc.scalar.activation(kf[0:TB, :], ps[0:TB, 4, :], ACT.Copy, scale=WS).then_inc(k_scaled, 1)

            def lot_hi(n):
                act.wait_ge(w2_turned, n + 1)
                nc.scalar.activation(act_gate, pcol, ACT.Copy)
                nc.scalar.activation(lot_target(n, 0), turned_tiles(n), ACT.Copy,
                                     scale=WS).then_inc(w2_hi, 1)

            def split_hi(i, m):
                n = 2 * STEPS * i + m
                act.wait_ge(x_loaded[m % 4], 4 * 16 * i + 16 * (m // 4 + 1))
                at_least(act, s0_summed, n - 1)
                nc.scalar.activation(xh[:, m % 2, :, ::-1], xin[:, m % 4], ACT.Copy, scale=XS).then_inc(x_hi, 1)

            def copy_left(i, m):
                k, g = m // STEPS, m % STEPS
                if g == 0:
                    for part in range(NPART):
                        at_least(act, x1_stored[k][part], 16 * i)
                act.wait_ge(s0_summed, 2 * STEPS * i + m + 1)
                nc.scalar.activation(xq[:, k, :, 16 * g:16 * g + 8], ps[:, 2 * (m % 2), :].rearrange("p (b d) -> p d b", d=C),
                                     ACT.Copy).then_inc(s0_left_out, 1)

            def stage0(i, first):
                for m in range(2 * STEPS):
                    k, step = m // STEPS, m % STEPS
                    blk = 2 * i + k
                    split_hi(i, m)
                    if m:
                        copy_left(i, m - 1)
                    if first and k == 0:
                        if step == 1:
                            load_lot(LOT_A)
                        if step == 2:
                            param_sines()
                            lot_hi(LOT_B)
                        if step == 4:
                            load_lot(LOT_W)
                        if step == 5:
                            copy_turned()
                            lot_hi(LOT_A)
                        if step == 7:
                            lot_hi(LOT_W)
                            chunk_sines(0)
                            scale_k(0)
                    else:
                        if step == 0:
                            load_lot(blk + LOT_W)
                        if step == 2:
                            store_k(blk - 1)
                        if step == 3:
                            chunk_sines(blk)
                        if step == 5:
                            lot_hi(blk + LOT_W)
                        if step == 7:
                            scale_k(blk)
                copy_left(i, 2 * STEPS - 1)

            stage0(0, True)
            with act.Fori(1, NBLK // 2) as i:
                stage0(i, False)
            store_k(NBLK - 1)

            def x1_split_hi(g, h):
                act.wait_ge(x1_loaded[h], 16 * (g + 1))
                nc.scalar.activation(x1h[:, h], x1f[:, h], ACT.Copy, scale=XS / FS).then_inc(x1_hi, 1)

            def x2_split_hi(g, h):
                act.wait_ge(c1_out, HG * g + h + 1)
                nc.scalar.activation(x2h[:, h], x1f[:, h], ACT.Copy, scale=XS / FS).then_inc(x2_hi, 1)

            for h in range(HG):
                x1_split_hi(0, h)
            for h in range(HG):
                x2_split_hi(0, h)
            for h in range(HG):
                x1_split_hi(1, h)

            def body(g, more1, more2):
                act.wait_ge(low_scaled, g + 1)
                nc.scalar.activation(lowh.rearrange("p (h b) -> p h b", h=HG), lowf, ACT.Copy).then_inc(low_hi, 1)
                for o in range(NBLK):
                    act.wait_ge(s2_summed, NBLK * g + o + 1)
                    nc.scalar.activation(x3h[:, :, o, :], ps[:, 4 + o % 3, :].rearrange("p (h b) -> p h b", h=HG), ACT.Identity,
                                         bias=biasx[:, o:o + 1], scale=XS / FS).then_inc(x3_hi, 1)
                if more1:
                    for h in range(HG):
                        x2_split_hi(g + 1, h)
                for h in range(HG):
                    act.wait_ge(c3_summed, HG * g + h + 1)
                    at_least(act, out_stored[h], 16 * g)
                    nc.scalar.activation(outt[:, h].rearrange("p (n c) -> p n c", n=2), ps[:, 2 * (h % 2):2 * (h % 2) + 2, :],
                                         ACT.Copy, scale=1.0 / FS).then_inc(c3_out, 1)
                    if more2:
                        x1_split_hi(g + 2, h)

            body(0, True, True)
            with act.Fori(1, NG - 2) as g:
                body(g, True, True)
            body(NG - 2, True, False)
            body(NG - 1, False, False)

        @block.vector
        def _(dve):
            step = [0]

            def link(ins):
                step[0] += 1
                ins.then_inc(dve_step, 1)
                dve.wait_ge(dve_step, step[0])

            ts, tt, stt = nc.vector.tensor_scalar, nc.vector.tensor_tensor, nc.vector.scalar_tensor_tensor

            dve.wait_ge(iota_done, 3)
            dve.wait_ge(ids_loaded, 64)
            nc.vector.tensor_copy(idf[:, :, :], ids[:, :, :])
            link(nc.vector.tensor_copy(pcol, pcoli))
            ts(onehot[:, :], idf[0:NID, 0, :], pcol[0:NID, :], None, ALU.is_equal)
            dve.wait_ge(w0_loaded, 16)
            diag = w0n[0:NID, 0:C * C]
            diag = bass.AP(diag.tensor, diag.offset, [diag.ap[0], [C + 1, C]])
            ts(diag, diag, 1.0, None, ALU.add).then_inc(w0_ready, 1)
            nc.vector.tensor_copy(tcol, tcoli)
            nc.vector.tensor_copy(trow[:, :], trowi[:, :])
            link(nc.vector.tensor_copy(len3f, len3i))
            for k in range(NBLK):
                ts(mask1[:, k, :], idf[:, 1, :], tcol[:, k:k + 1], None, ALU.is_gt).then_inc(masks_ready, 1)
            dve.wait_ge(w0_hi, 1)
            stt(w0l[0:NID, :], w0n[0:NID, :], WS, w0h[0:NID, :], ALU.mult, ALU.subtract).then_inc(w0_lo, 1)
            ts(past3[:, :], trow[:, :], len3f, None, ALU.is_ge).then_inc(masks_ready, 1)
            link(ts(rank_adapter, pcol, 1.0 / RANK, -0.5 + 0.5 / RANK, ALU.mult, ALU.add))
            link(ts(rank_adapter, rank_adapter, ROUND, ROUND, ALU.add, ALU.subtract))
            dve.wait_ge(consts_loaded, 16 * (NADAPT + 1))
            link(ts(rank_scale, rank_scale, XS / FS, None, ALU.mult))
            ts(adapter_scale[:, :], idf[:, 2, :], rank_adapter, rank_scale, ALU.is_equal, ALU.mult)
            nc.vector.tensor_copy(bias_rev[0:NBLK, ::-1], biasn[0:NBLK, :])
            link(ts(quarter_own, pcol, float(C), 0.25, ALU.is_lt, ALU.mult))
            link(ts(quarter_oth, quarter_own, -1.0, 0.25, ALU.mult, ALU.add))
            for n, (half, quarter) in enumerate(((half_own, quarter_own), (half_oth, quarter_oth))):
                ts(half[:, 0:1], quarter, 0.5, None, ALU.subtract)
                ts(half[:, 1:2], quarter, 0.5, None, ALU.add)
            link(ts(phase_own, quarter_own, 2 * math.pi, None, ALU.mult))
            link(ts(phase_oth, quarter_oth, 2 * math.pi, None, ALU.mult))
            dve.wait_ge(pick_cleared, 1)
            for dgroup in range(8):
                dve.wait_ge(pick_summed, 2 * dgroup + 2)
                for q in range(2):
                    rows = slice(q * C, (q + 1) * C)
                    e = nc.vector.tensor_copy(pick[rows, :, 1, q * C + 8 * dgroup:q * C + 8 * dgroup + 8],
                                              ps[rows, (2 * dgroup + 1) % 8, :].rearrange("p (e n) -> p n e", e=8))
                e.then_inc(pick_lo_copied, 1)

            def col(n, w=64):
                return prm[:, 64 * n:64 * n + w]

            def exp_exact(dst, src, w, t1, t2, t3):
                link(ts(t1, src, 1.0 / math.log(2.0), ROUND, ALU.mult, ALU.add))
                link(ts(t1, t1, ROUND, None, ALU.subtract))
                link(stt(t2, t1, -LN2_HI, src, ALU.mult, ALU.add))
                link(stt(t2, t1, -LN2_LO, t2, ALU.mult, ALU.add))
                link(ts(t3, t2, 1.0 / 5040, None, ALU.mult))
                for c in (720, 120, 24, 6, 2, 1):
                    link(stt(t3, t3, 1.0 / c, t2, ALU.add, ALU.mult))
                link(ts(t3, t3, 1.0, None, ALU.add))
                link(ts(t1.bitcast(I32), t1, 127.0, 8388608.0, ALU.add, ALU.mult))
                link(tt(dst, t3, t1, ALU.mult))

            def turns(dst, src, tmp, quarter, phase):
                link(ts(tmp, src, 1.0 / (2 * math.pi), quarter, ALU.mult, ALU.add))
                link(ts(tmp, tmp, ROUND, ROUND, ALU.add, ALU.subtract))
                link(stt(dst, tmp, -TWO_PI_HI, src, ALU.mult, ALU.add))
                link(stt(dst, tmp, -TWO_PI_LO, dst, ALU.mult, ALU.add))
                link(ts(dst, dst, phase, PI_CLAMP, ALU.add, ALU.min))
                link(ts(dst, dst, -PI_CLAMP, None, ALU.max))

            dt = prm[:, 448:449]
            t = [col(n) for n in range(16, 32)]
            ar, ai = t[0], col(2)
            re, im = col(8), col(9)

            def params_first():
                dve.wait_ge(ssm_loaded, 160)
                exp_exact(prm[:, 448:449], prm[:, 0:1], 1, prm[:, 449:450], prm[:, 450:451], prm[:, 451:452])
                exp_exact(t[0], col(1), 64, t[1], t[2], t[3])
                link(ts(re, ar, dt, -1.0, ALU.mult, ALU.mult))
                link(ts(im, ai, dt, None, ALU.mult))
                link(ts(ar, ar, -1.0, None, ALU.mult))
                link(ts(t[4], im, 0.5, None, ALU.mult))
                turns(col(10), im, t[5], 0.0, 0.0)
                link(ts(col(14), col(10), 1.0 / (2 * math.pi), None, ALU.mult))
                turns(col(11), im, t[5], 0.25, math.pi / 2)
                turns(col(12), t[4], t[5], 0.0, 0.0)
                exp_exact(t[6], re, 64, t[1], t[2], t[3])
                tt(t[5], ar, ar, ALU.mult).then_inc(angles_ready, 1)
                link(tt(t[4], ai, ai, ALU.mult))
                link(tt(t[4], t[4], t[5], ALU.add))
                link(nc.vector.reciprocal(t[7], t[4]))

            def params_rest():
                dve.wait_ge(sines_ready, 2)
                sin, cos, sinh2, tanh = col(10), col(11), col(12), col(13)
                link(ts(t[1], t[6], 1.0, None, ALU.add))
                link(tt(t[1], t[1], tanh, ALU.mult))
                link(tt(t[1], t[1], cos, ALU.mult))
                link(tt(t[2], sinh2, sinh2, ALU.mult))
                link(stt(t[1], t[2], -2.0, t[1], ALU.mult, ALU.add))
                link(tt(t[2], t[6], sin, ALU.mult))
                cr = prm[:, 192:320].rearrange("p (n r) -> p r n", r=2)[:, 0, :]
                ci = prm[:, 192:320].rearrange("p (n r) -> p r n", r=2)[:, 1, :]

                def complex_mult(o_re, o_im, a_re, a_im, b_re, b_im, t1):
                    link(tt(o_re, a_re, b_re, ALU.mult))
                    link(tt(t1, a_im, b_im, ALU.mult))
                    link(tt(o_re, o_re, t1, ALU.subtract))
                    link(tt(o_im, a_re, b_im, ALU.mult))
                    link(tt(t1, a_im, b_re, ALU.mult))
                    link(tt(o_im, o_im, t1, ALU.add))

                complex_mult(t[8], t[9], cr, ci, t[1], t[2], t[3])
                link(ts(t[10], ai, -1.0, None, ALU.mult))
                complex_mult(t[11], t[12], t[8], t[9], ar, t[10], t[3])
                link(tt(t[11], t[11], t[7], ALU.mult))
                link(tt(t[12], t[12], t[7], ALU.mult))
                big = prm[:, 1024:1536]
                nc.vector.tensor_copy(big[:, 0:64], re)
                nc.vector.tensor_copy(big[:, 64:128], re)
                nc.vector.tensor_copy(big[:, 128:192], col(14))
                nc.vector.tensor_copy(big[:, 192:256], col(14))
                ts(big[:, 256:320], t[11], 2.0, None, ALU.mult)
                ts(big[:, 320:384], t[11], -2.0, None, ALU.mult)
                ts(big[:, 384:448], t[12], -2.0, None, ALU.mult)
                ts(big[:, 448:512], t[12], -2.0, None, ALU.mult)
                ts(d_row[0:1, :], prm[0:1, 320:448], 1.0, WS, ALU.add, ALU.mult).then_inc(params_ready, 1)

            right_l = trow[:, 0:TB].rearrange("p (o l) -> p o l", o=1).to_broadcast([P, CH, TB])
            left_l = trow.rearrange("p (o l s) -> p o l s", o=1, s=TB)[:, :, :, 0].to_broadcast([P, CH, TB])
            NLINK = 16

            def table_link(ins, c, n):
                ins.then_inc(table_step, 1)
                dve.wait_ge(table_step, NLINK * c + n)

            def param(c, n):
                return turned[:, n, bass.ds(c * CH, CH)].rearrange("p (h o) -> p h o", o=1).to_broadcast([P, CH, TB])

            def round_off(tile, angle, quarter, half, c, n):
                table_link(ts(tile, angle, quarter, ROUND, ALU.add, ALU.add), c, n)
                table_link(stt(tile, tile, ROUND, angle, ALU.subtract, ALU.subtract), c, n + 1)
                table_link(ts(tile, tile, half[:, 0:1], half[:, 1:2], ALU.max, ALU.min), c, n + 2)

            def right_angles(c):
                at_least(dve, k_summed, c)
                table_link(tt(wide(angle_r), param(c, 1), right_l, ALU.mult), c, 1)
                round_off(turn_r, angle_r, quarter_own, half_own, c, 2)

            def left_angles(c):
                table_link(tt(wide(angle_l), param(c, 1), left_l, ALU.mult), c, 5)
                round_off(turn_own, angle_l, quarter_own, half_own, c, 6)
                round_off(turn_oth, angle_l, quarter_oth, half_oth, c, 9)

            def decays(c):
                tt(wide(angle_r), param(c, 0), right_l, ALU.mult)
                tt(wide(angle_l), param(c, 0), left_l, ALU.mult).then_inc(table_angles, 1)

            def combine(c):
                dve.wait_ge(table_sines, c + 1)
                table_link(tt(turn_r, turn_r, angle_r, ALU.mult), c, 12)
                table_link(tt(wide(turn_own), wide(turn_own), param(c, 2), ALU.mult), c, 13)
                table_link(tt(wide(turn_oth), wide(turn_oth), param(c, 3), ALU.mult), c, 14)
                table_link(tt(turn_own, turn_own, turn_oth, ALU.add), c, 15)
                tt(turn_own, turn_own, angle_l, ALU.mult).then_inc(tables_ready, 1)

            def split_k(c):
                dve.wait_ge(k_scaled, c + 1)
                dve.wait_ge(krow_stored, 32 * c + 16)
                k0 = wide(kf)[0:1, :, 0]
                table_link(tt(k0, k0, d_row[0:1, bass.ds(c * CH, CH)], ALU.add), c, 16)
                nc.vector.tensor_copy(kh[0:TB, :], kf[0:TB, :]).then_inc(k_hi, 1)
                dve.wait_ge(k_hi, c + 1)
                tt(kl[0:TB, :], kf[0:TB, :], kh[0:TB, :], ALU.subtract).then_inc(k_split, 1)

            def lot_ready(n):
                dve.wait_ge(wrow_loaded, 16 * (NADAPT + n))
                at_least(dve, w2_turned, n)
                src = wrow.rearrange("p (m i) -> p m i", m=NBLK)
                dst = wrow_rev.rearrange("p (m i) -> p m i", m=NBLK)
                if isinstance(n, int) and n == LOT_B:
                    nc.vector.tensor_copy(wrow_rev, wrow).then_inc(w2_ready, 1)
                elif isinstance(n, int) and n == LOT_A:
                    nc.vector.tensor_copy(dst[:, :, ::-1], src).then_inc(w2_ready, 1)
                else:
                    nc.vector.tensor_copy(dst[:, :, ::-1], src).then_inc(w2_rev, 1)
                    dve.wait_ge(w2_rev, n - LOT_W + 1)
                    own = wrow_rev[:, bass.ds((n - LOT_W) * P, P)]
                    stt(own, flip[:, :], XS, own, ALU.mult, ALU.add).then_inc(w2_ready, 1)

            def lot_lo(n):
                dve.wait_ge(w2_hi, n + 1)
                stt(lot_target(n, 1), turned_tiles(n), WS, lot_target(n, 0),
                    ALU.mult, ALU.subtract).then_inc(w2_lo, 1)

            def split_lo(i, m):
                dve.wait_ge(x_hi, 2 * STEPS * i + m + 1)
                stt(xl[:, m % 2, :, ::-1], xin[:, m % 4], XS, xh[:, m % 2, :, ::-1], ALU.mult, ALU.subtract).then_inc(x_lo, 1)

            def copy_right(i, m):
                k, g = m // STEPS, m % STEPS
                if g == 0:
                    for part in range(NPART):
                        at_least(dve, x1_stored[k][part], 16 * i)
                dve.wait_ge(s0_summed, 2 * STEPS * i + m + 1)
                nc.vector.tensor_copy(xq[:, k, :, 16 * g + 8:16 * g + 16],
                                      ps[:, 2 * (m % 2) + 1, :].rearrange("p (b d) -> p d b", d=C)).then_inc(s0_right_out, 1)

            def turned_bias():
                dve.wait_ge(params_turned, 1)
                ts(biasx[:, :], ps[:, 5, 0:NBLK], XS, None, ALU.mult)
                dve.wait_ge(turned_copied, 1)

            def stage0(i, first):
                for m in range(2 * STEPS):
                    k, step = m // STEPS, m % STEPS
                    blk = 2 * i + k
                    split_lo(i, m)
                    if m:
                        copy_right(i, m - 1)
                    if first and k == 0:
                        if step == 0:
                            lot_ready(LOT_B)
                        if step == 1:
                            params_first()
                        if step == 2:
                            lot_lo(LOT_B)
                        if step == 3:
                            params_rest()
                            lot_ready(LOT_A)
                        if step == 5:
                            lot_lo(LOT_A)
                            lot_ready(LOT_W)
                        if step == 7:
                            lot_lo(LOT_W)
                            turned_bias()
                            right_angles(0)
                            left_angles(0)
                            decays(0)
                            combine(0)
                            split_k(0)
                    else:
                        if step == 0:
                            right_angles(blk)
                        if step == 1:
                            left_angles(blk)
                        if step == 2:
                            decays(blk)
                        if step == 3:
                            lot_ready(blk + LOT_W)
                        if step == 4:
                            combine(blk)
                        if step == 6:
                            lot_lo(blk + LOT_W)
                        if step == 7:
                            split_k(blk)
                copy_right(i, 2 * STEPS - 1)

            stage0(0, True)
            with dve.Fori(1, NBLK // 2) as i:
                stage0(i, False)

            def turn_g1(g, h):
                dve.wait_ge(g1_loaded[h], 16 * (g + 1))
                at_least(dve, c1_summed, HG * (g - 1) + h + 1)
                nc.vector.tensor_copy(g1[:, h].rearrange("p s (d t) -> p (s d) t", t=P)[:, :, ::-1],
                                      g1n[:, h % 2].rearrange("p s (d t) -> p (s d) t", t=P)).then_inc(g1_turned, 1)

            gate = small[:, 40:40 + 2 * HG]
            dve.wait_ge(masks_ready, NBLK + 1)
            def x1_split_lo(g, h):
                dve.wait_ge(x1_hi, HG * g + h + 1)
                stt(x1l[:, h], x1f[:, h], XS / FS, x1h[:, h], ALU.mult, ALU.subtract).then_inc(x1_lo, 1)

            def take_conv1(g, h):
                dve.wait_ge(c1_summed, HG * g + h + 1)
                nc.vector.memset(gate[:, h:h + 1], 0.0)
                b0 = 2 * (h % 2)
                nc.vector.copy_predicated(x1f[:, h].rearrange("p k b -> p (k b)"), mask1[:, :, :].rearrange("p k b -> p (k b)"),
                                          ps[:, b0:b0 + 2, :].rearrange("p n c -> p (n c)")).then_inc(c1_out, 1)

            def x2_split_lo(g, h):
                dve.wait_ge(x2_hi, HG * g + h + 1)
                stt(x2l[:, h], x1f[:, h], XS / FS, x2h[:, h], ALU.mult, ALU.subtract).then_inc(x2_lo, 1)

            def conv1(g):
                for h in range(HG):
                    take_conv1(g, h)
                    if h:
                        x2_split_lo(g, h - 1)
                x2_split_lo(g, HG - 1)

            for h in range(HG):
                turn_g1(0, h)
            for h in range(HG):
                x1_split_lo(0, h)
            conv1(0)
            for h in range(HG):
                turn_g1(1, h)
                x1_split_lo(1, h)

            def body(g, more1, more2):
                dve.wait_ge(low_summed, g + 1)
                tt(lowf, ps[:, 7, :].rearrange("p (h b) -> p h b", h=HG),
                   adapter_scale[:, :].rearrange("p (o b) -> p o b", o=1).to_broadcast([P, HG, B]), ALU.mult).then_inc(low_scaled, 1)
                dve.wait_ge(low_hi, g + 1)
                tt(lowl.rearrange("p (h b) -> p h b", h=HG), lowf, lowh.rearrange("p (h b) -> p h b", h=HG),
                   ALU.subtract).then_inc(low_lo, 1)

                def lo3(o):
                    dve.wait_ge(s2_out, NBLK * g + o + 1)
                    tt(x3l[:, :, o, :], x3f[:, o % 2], x3h[:, :, o, :], ALU.subtract).then_inc(x3_lo, 1)

                for o in range(NBLK):
                    if o >= 2:
                        dve.wait_ge(x3_lo, NBLK * g + o - 1)
                    dve.wait_ge(x3_hi, NBLK * g + o + 1)
                    ts(x3f[:, o % 2], ps[:, 4 + o % 3, :].rearrange("p (h b) -> p h b", h=HG), XS / FS, biasx[:, o:o + 1],
                       ALU.mult, ALU.add).then_inc(s2_out, 1)
                    if o:
                        lo3(o - 1)
                lo3(NBLK - 1)
                if more1:
                    conv1(g + 1)
                for h in range(HG):
                    dve.wait_ge(c3_out, HG * g + h + 1)
                    nc.vector.memset(gate[:, HG + h:HG + h + 1], 0.0)
                    t0 = 4 + 2 * (h % 2)
                    nc.vector.copy_predicated(outt[:, h], past3[:, :],
                                              ps[:, t0:t0 + 2, :].rearrange("p n c -> p (n c)")).then_inc(c3_past, 1)
                    if more2:
                        turn_g1(g + 2, h)
                        x1_split_lo(g + 2, h)

            body(0, True, True)
            with dve.Fori(1, NG - 2) as g:
                body(g, True, True)
            body(NG - 2, True, False)
            body(NG - 1, False, False)


_INS = ['x', 'itok_B_0_15', 'itok_B_78_3631', 'itok_B_1_7', 'itok_B_8_3872', 'L0_cond_weights',
        'L1_cond_log_dt', 'L1_cond_C', 'L1_cond_log_A_real', 'L1_cond_A_imag', 'L1_cond_D',
        'L2_cond_weight', 'L2_cond_bias', 'L2_cond_lora_a_weights', 'L2_cond_lora_b_weights', 'L2_cond_scaling_factors',
        'L3_cond_log_dt', 'L3_cond_C', 'L3_cond_log_A_real', 'L3_cond_A_imag', 'L3_cond_D']


def kernel(**inputs):
    import numpy as _np
    import concourse.bacc as _bacc
    from concourse import mybir as _mybir
    from concourse.bass_utils import run_bass_kernel_spmd as _run

    nc = _bacc.Bacc("TRN2", target_bir_lowering=False, num_devices=1)
    arrays, ap = {}, {}
    for name in _INS:
        a = _np.ascontiguousarray(inputs[name])
        arrays[f"in_{name}_dram"] = a
        ap[name] = nc.dram_tensor(f"in_{name}_dram", a.shape, _mybir.dt.from_np(a.dtype), kind="ExternalInput").ap()
    out = nc.dram_tensor("out_0_dram", (B, C, T), _mybir.dt.float32, kind="ExternalOutput").ap()

    def ssm(p):
        return tuple(ap[f"{p}_cond_{n}"] for n in ("log_dt", "C", "log_A_real", "A_imag", "D"))

    build(nc, ap['x'], ap['itok_B_0_15'], ap['itok_B_78_3631'], ap['itok_B_1_7'], ap['itok_B_8_3872'],
          ap['L0_cond_weights'], ssm("L1"), ssm("L3"), ap['L2_cond_weight'], ap['L2_cond_bias'],
          ap['L2_cond_lora_a_weights'], ap['L2_cond_lora_b_weights'], ap['L2_cond_scaling_factors'], out)
    r = _run(nc, [arrays], core_ids=[0])
    return r.results[0]["out_0_dram"]
```

```python
import math
from contextlib import ExitStack

import concourse.bass as bass
from concourse import mybir

ALU = mybir.AluOpType
ACT = mybir.ActivationFunctionType
F32 = mybir.dt.float32
F16 = mybir.dt.float16
I32 = mybir.dt.int32
U8 = mybir.dt.uint8

P = 128
B, C, T = 128, 64, 1024
NBLK = T // P
NID, NADAPT, RANK = 16, 8, 16
XS, WS = 32.0, 64.0
FS = XS * WS
PAIRS = B // 2
NXIN = 8
GPAIRS = 4
STEPS = PAIRS // GPAIRS
NXH = 4
NPART = 4
HG = 4
NG = C // HG
TB = 32
CH = 2 * C // NBLK
KROW = P + T

ROUND = 12582912.0
TWO_PI_HI = 6.28125
TWO_PI_LO = 2 * math.pi - TWO_PI_HI
LN2_HI = 0.693359375
LN2_LO = math.log(2.0) - LN2_HI
PI_CLAMP = 3.1415925
TURN = 6.2831845


def at_least(engine, semaphore, value):
    if not (isinstance(value, int) and value <= 0):
        engine.wait_ge(semaphore, value)


def build(nc, x, ids0, len1, ids2, len3, w0, ssm1, ssm3, w2, bias2, lora_a, lora_b, lora_s, out):
    with ExitStack() as ctx:
        def sem(name):
            return ctx.enter_context(nc.semaphore(name))

        def sb(name, shape, dt):
            return ctx.enter_context(nc.sbuf_tensor(name, shape, dt))

        x1_dram = nc.dram_tensor("x1_scratch", [NBLK, P, C, B], F32).ap()
        krow_t = nc.dram_tensor("krow_scratch", [2, C, 2, KROW], F16)
        krow = krow_t.ap()

        ps = ctx.enter_context(nc.psum_tensor("ps", [P, 8, 512], F32))

        ident = sb("ident", [P, P], F32)
        w2t = sb("w2t", [P, 2, NBLK, T], F16)
        at = sb("at", [P, 2, NBLK, P], F16)
        bt = sb("bt", [P, 2, T], F16)
        adapter_scale = sb("adapter_scale", [P, B], F32)
        biasx = sb("biasx", [P, NBLK], F32)
        mask1 = sb("mask1", [P, NBLK, B], U8)
        past3 = sb("past3", [P, T], U8)
        flip = sb("flip", [P, P], F16)
        gbuf = sb("gbuf", [P, 40 * 256], F32)

        def part_of(tile, at_kb, kb, dt=F32):
            v = tile[:, int(at_kb * 256):int((at_kb + kb) * 256)]
            return v if dt == F32 else v.bitcast(dt)

        x1f = part_of(gbuf, 0, 16).rearrange("p (h k b) -> p h k b", h=HG, k=NBLK)
        g1 = part_of(gbuf, 16, 16, F16).rearrange("p (h s t) -> p h s t", h=HG, s=2)
        g1n = part_of(gbuf, 32, 8, F16).rearrange("p (h s t) -> p h s t", h=2, s=2)
        prm = part_of(gbuf, 0, 8)
        angle_r, angle_l, turn_r, turn_own, turn_oth = [part_of(gbuf, 16 + 2 * n, 2) for n in range(5)]
        turned = part_of(gbuf, 26, 2).rearrange("p (n r) -> p n r", n=4)
        kf = part_of(gbuf, 28, 2)
        kh = part_of(gbuf, 30, 1, F16)
        kl = part_of(gbuf, 31, 1, F16)
        wrow = part_of(gbuf, 32, 4)
        wrow_rev = part_of(gbuf, 36, 4)
        small = sb("small", [P, 64], F32)
        steps = sb("steps", [P, 2 * TB], F32)
        d_row = sb("d_row", [1, 2 * C], F32)

        arena = sb("arena", [P, 120 * 256], F32)

        def area(at_kb, kb, dt=F32):
            return part_of(arena, at_kb, kb, dt)

        pick = area(0, 32, F16).rearrange("p (n s d) -> p n s d", n=PAIRS, s=2)
        xin = area(32, 16).rearrange("p (s n t) -> p s n t", s=NXIN, n=GPAIRS)
        xh = area(48, 4, F16).rearrange("p (s n t) -> p s n t", s=NXH, n=GPAIRS)
        xl = area(52, 4, F16).rearrange("p (s n t) -> p s n t", s=NXH, n=GPAIRS)
        xq = area(56, 64).rearrange("p (k d b) -> p k d b", k=2, d=C)
        w0n = area(56, 16)
        w0h = area(72, 8, F16)
        w0l = area(80, 8, F16)
        trow = area(88, 4)
        trowi = area(92, 4, I32)
        ids = area(96, 1.5, I32).rearrange("p (n b) -> p n b", n=3)
        idf = area(97.5, 1.5).rearrange("p (n b) -> p n b", n=3)
        biasn = area(99, 0.5)
        bias_rev = area(99.5, 0.5)
        g3 = area(0, 16, F16).rearrange("p (h s t) -> p h s t", h=HG, s=2)
        x1h = area(16, 8, F16).rearrange("p (h k b) -> p h k b", h=HG, k=NBLK)
        x1l = area(24, 8, F16).rearrange("p (h k b) -> p h k b", h=HG, k=NBLK)
        x2h = area(32, 8, F16).rearrange("p (h k b) -> p h k b", h=HG, k=NBLK)
        x2l = area(40, 8, F16).rearrange("p (h k b) -> p h k b", h=HG, k=NBLK)
        x3h = area(48, 8, F16).rearrange("p (h k b) -> p h k b", h=HG, k=NBLK)
        x3l = area(56, 8, F16).rearrange("p (h k b) -> p h k b", h=HG, k=NBLK)
        outt = area(64, 16).rearrange("p (h t) -> p h t", h=HG)
        x3f = area(80, 4).rearrange("p (s h b) -> p s h b", s=2, h=HG)
        lowf = area(84, 2).rearrange("p (h b) -> p h b", h=HG)
        lowh = area(86, 1, F16)
        lowl = area(87, 1, F16)
        x3t = area(88, 16, F16).rearrange("p (h s k t) -> p h s k t", h=HG, s=2, k=NBLK)
        past = area(104, 8).rearrange("p (s t) -> p s t", s=2)

        half_own = small[:, 10:12]
        half_oth = small[:, 12:14]
        act_gate = small[:, 48:49]
        pcol = small[:, 0:1]
        phase_own = small[:, 1:2]
        phase_oth = small[:, 2:3]
        quarter_own = small[:, 3:4]
        quarter_oth = small[:, 4:5]
        rank_scale = small[:, 5:6]
        rank_adapter = small[:, 6:7]
        len3f = small[:, 7:8]
        len3i = small[:, 8:9].bitcast(I32)
        pcoli = small[:, 9:10].bitcast(I32)
        tcol = small[:, 16:24]
        tcoli = small[:, 24:32].bitcast(I32)
        onehot = sb("onehot", [NID, B], F16)
        zrow = sb("zrow", [P, P], F32)
        one_xs = sb("one_xs", [P, 1], F32)

        consts_loaded = sem("consts_loaded")
        iota_done = sem("iota_done")
        ids_loaded = sem("ids_loaded")
        w0_loaded = sem("w0_loaded")
        ssm_loaded = sem("ssm_loaded")
        dve_step = sem("dve_step")
        table_step = sem("table_step")
        masks_ready = sem("masks_ready")
        params_ready = sem("params_ready")
        params_turned = sem("params_turned")
        turned_copied = sem("turned_copied")
        angles_ready = sem("angles_ready")
        sines_ready = sem("sines_ready")
        table_angles = sem("table_angles")
        table_sines = sem("table_sines")
        tables_ready = sem("tables_ready")
        k_summed = sem("k_summed")
        k_scaled = sem("k_scaled")
        d_added = sem("d_added")
        k_hi = sem("k_hi")
        k_split = sem("k_split")
        krow_stored = sem("krow_stored")
        zeros_ready = sem("zeros_ready")
        w0_ready = sem("w0_ready")
        w0_hi = sem("w0_hi")
        w0_lo = sem("w0_lo")
        pick_cleared = sem("pick_cleared")
        pick_summed = sem("pick_summed")
        pick_hi_copied = sem("pick_hi_copied")
        pick_lo_copied = sem("pick_lo_copied")
        x_loaded = [sem(f"x_loaded{s}") for s in range(NXIN)]
        x_hi = sem("x_hi")
        x_lo = sem("x_lo")
        s0_summed = sem("s0_summed")
        s0_even_out = sem("s0_even_out")
        s0_odd_out = sem("s0_odd_out")
        x1_kept = sem("x1_kept")
        x1_stored = [[sem(f"x1_stored{k}{part}") for part in range(NPART)] for k in range(2)]
        wrow_loaded = sem("wrow_loaded")
        w2_rev = sem("w2_rev")
        w2_ready = sem("w2_ready")
        w2_turned = sem("w2_turned")
        w2_hi = sem("w2_hi")
        w2_lo = sem("w2_lo")
        x1_loaded = [sem(f"x1_loaded{h}") for h in range(HG)]
        g1_loaded = [sem(f"g1_loaded{h}") for h in range(HG)]
        g3_loaded = [sem(f"g3_loaded{h}") for h in range(HG)]
        out_stored = [sem(f"out_stored{h}") for h in range(HG)]
        x1_hi = sem("x1_hi")
        x1_lo = sem("x1_lo")
        g1_turned = sem("g1_turned")
        c1_summed = sem("c1_summed")
        c1_out = sem("c1_out")
        x2_hi = sem("x2_hi")
        x2_lo = sem("x2_lo")
        low_summed = sem("low_summed")
        low_scaled = sem("low_scaled")
        low_hi = sem("low_hi")
        low_lo = sem("low_lo")
        s2_summed = sem("s2_summed")
        x3_hi = sem("x3_hi")
        s2_out = sem("s2_out")
        x3_lo = sem("x3_lo")
        c3_summed = sem("c3_summed")
        c3_out = sem("c3_out")
        c3_past = sem("c3_past")
        x3_turned = [sem(f"x3_turned{h}") for h in range(HG)]
        past_summed = sem("past_summed")
        past_ready = sem("past_ready")

        ssm = (ssm1, ssm3)
        NLINK = 15
        LOT_B, LOT_A, LOT_W = 0, 1, 2

        x_pairs = x.rearrange("(n q) c t -> (q c) n t", q=2)

        def lot_target(n, part):
            if isinstance(n, int) and n == LOT_B:
                return bt[:, part, :].rearrange("p (m o) -> p m o", m=NBLK)
            if isinstance(n, int) and n == LOT_A:
                return at[:, part, :, :]
            return w2t[:, part, :, bass.ds((n - LOT_W) * P, P)]

        def turned_tiles(n):
            tiles = ps[:, 6:8, :].rearrange("p q (m o) -> p (q m) o", m=4)
            return tiles if isinstance(n, int) and n == LOT_A else tiles[:, :, ::-1]

        def half_cols(tile, half):
            return tile[0:NID, :].rearrange("i (c d) -> i c d", d=C)[:, :, half * (C // 2):(half + 1) * (C // 2)]

        def wide(tile):
            return tile.rearrange("p (h l) -> p h l", h=CH)

        block = ctx.enter_context(nc.Block())

        @block.sync
        def _(sp):
            for n, row in enumerate((ids0, len1, ids2)):
                sp.dma_start(ids[:, n, :], row.rearrange("(o b) -> o b", o=1).to_broadcast([P, B])).then_inc(ids_loaded, 16)
            sp.dma_start(len3i, len3.rearrange("(b o) -> b o", o=1)).then_inc(ids_loaded, 16)
            for quarter in range(4):
                cols = slice(quarter * (C * C // 4), (quarter + 1) * (C * C // 4))
                sp.dma_start(w0n[0:NID, cols], w0.rearrange("i c d -> i (c d)")[:, cols]).then_inc(w0_loaded, 16)

            def load_x(i, m):
                k, g = m // STEPS, m % STEPS
                n = 2 * STEPS * i + m
                at_least(sp, x_hi, n - NXIN + 1)
                at_least(sp, x_lo, n - NXIN + 1)
                t0 = (2 * i + k) * P
                sp.dma_start(xin[:, m % NXIN], x_pairs[:, g * GPAIRS:(g + 1) * GPAIRS, bass.ds(t0, P)]).then_inc(x_loaded[m % NXIN], 16)

            def store_x1(i, k, part):
                sp.wait_ge(s0_even_out, (2 * i + k + 1) * (STEPS // 2))
                sp.wait_ge(s0_odd_out, (2 * i + k + 1) * (STEPS // 2))
                d0, d1 = max(HG, part * (C // NPART)), (part + 1) * (C // NPART)
                sp.dma_start(x1_dram[bass.ds(2 * i + k, 1), :, d0:d1, :].rearrange("o p d b -> (o p) (d b)"),
                             xq[:, k, d0:d1].rearrange("p d b -> p (d b)")).then_inc(x1_stored[k][part], 16)

            STORE_AT = {6: 0, 8: 1, 12: 2, 14: 3}

            def stage0(i, first):
                for m in range(2 * STEPS):
                    k, step = m // STEPS, m % STEPS
                    load_x(i, m)
                    if step in STORE_AT and not (first and k == 0):
                        store_x1(*((i, 0) if k else (i - 1, 1)), STORE_AT[step])

            stage0(0, True)
            with sp.Fori(1, NBLK // 2) as i:
                stage0(i, False)

            def load_g(v, g, h):
                tile = (g1n[:, h % 2], g3[:, h])[v]
                src = bass.AP(krow_t, (HG * g + h) * (2 * KROW) + v * (C * 2 * KROW) + 1, [[1, P], [KROW, 2], [1, T]])
                sp.dma_start(tile, src).then_inc((g1_loaded, g3_loaded)[v][h], 16)

            def load_x1(g, h):
                src = x1_dram.rearrange("k p d b -> p d k b")[:, bass.ds(HG * g + h, 1)].rearrange("p o k b -> p (o k) b")
                sp.dma_start(x1f[:, h], src).then_inc(x1_loaded[h], 16)

            def load_g1(g, h):
                at_least(sp, g1_turned, HG * g + h - 1)
                load_g(0, g, h)

            sp.wait_ge(krow_stored, 16 + 32)
            sp.wait_ge(w2_ready, LOT_W + NBLK)
            load_g1(0, 0)
            sp.wait_ge(w2_turned, LOT_W + NBLK)
            load_g1(0, 1)
            for part in range(NPART):
                store_x1(NBLK // 2 - 1, 1, part)
            for h in range(2, HG):
                load_g1(0, h)
            sp.wait_ge(s0_summed, NBLK * STEPS)
            sp.wait_ge(krow_stored, 16 + 32 * NBLK)
            for h in range(HG):
                load_g(1, 0, h)
            for part in range(NPART):
                for k in range(2):
                    sp.wait_ge(x1_stored[k][part], 16 * NBLK // 2)

            def reload_first(g, h, with_g1=True):
                if with_g1:
                    load_g1(g, h)
                sp.wait_ge(x2_hi, HG * (g - 1) + h + 1)
                sp.wait_ge(x2_lo, HG * (g - 1) + h + 1)
                load_x1(g, h)

            for h in range(HG):
                reload_first(1, h)

            def turn_x3(g, more2):
                sp.wait_ge(x3_hi, NBLK * (g + 1))
                sp.wait_ge(x3_lo, NBLK * (g + 1))
                if more2:
                    load_g1(g + 2, 0)
                for h in range(HG):
                    for part, xx in enumerate((x3h, x3l)):
                        sp.dma_start_transpose(x3t[:, h, part], xx[:, h].rearrange("p k b -> p (k b)")).then_inc(x3_turned[h], 16)

            def body(g, more1, more2):
                turn_x3(g, more2)
                if more2:
                    for h in range(HG):
                        reload_first(g + 2, h, h > 0)
                for h in range(HG):
                    sp.wait_ge(c3_past, HG * g + h + 1)
                    sp.dma_start(out[:, bass.ds(HG * g + h, 1), :].rearrange("b o t -> b (o t)"), outt[:, h]).then_inc(out_stored[h], 16)
                    if more1:
                        sp.wait_ge(c3_summed, HG * g + h + 1)
                        load_g(1, g + 1, h)

            body(0, True, True)
            with sp.Fori(1, NG - 2) as g:
                body(g, True, True)
            body(NG - 2, True, False)
            body(NG - 1, False, False)
            for h in range(HG):
                sp.wait_ge(out_stored[h], 16 * NG)

        @block.gpsimd
        def _(pool):
            nc.gpsimd.iota(pcoli, [[0, 1]], base=0, channel_multiplier=1).then_inc(iota_done, 1)
            nc.gpsimd.iota(tcoli, [[P, NBLK]], base=P - 1, channel_multiplier=-1).then_inc(iota_done, 1)
            nc.gpsimd.iota(trowi[:, 0:T], [[1, T]], base=0, channel_multiplier=0).then_inc(iota_done, 1)
            nc.gpsimd.memset(ident[:, :], 0.0).then_inc(iota_done, 1)
            nc.gpsimd.memset(flip[:, :], 0.0).then_inc(iota_done, 1)
            pool.wait_ge(iota_done, 5)
            nc.gpsimd.affine_select(out=ident[:, :], in_=ident[:, :], compare_op=ALU.not_equal, fill=1.0, base=0,
                                    pattern=[[-1, P]], channel_multiplier=1).then_inc(iota_done, 1)
            nc.gpsimd.affine_select(out=flip[:, :], in_=flip[:, :], compare_op=ALU.not_equal, fill=1.0 / XS, base=-(P - 1),
                                    pattern=[[1, P]], channel_multiplier=1).then_inc(iota_done, 1)
            nc.gpsimd.memset(zrow[:, :], 0.0).then_inc(zeros_ready, 1)
            nc.gpsimd.memset(one_xs[:, :], 1.0 / XS).then_inc(zeros_ready, 1)
            nc.gpsimd.memset(area(0, 32), 0.0).then_inc(pick_cleared, 1)

            def split_lo(i, m):
                pool.wait_ge(x_hi, 2 * STEPS * i + m + 1)
                nc.gpsimd.tensor_tensor(xl[:, m % NXH, :, ::-1], xin[:, m % NXIN], xh[:, m % NXH, :, ::-1],
                                        ALU.subtract).then_inc(x_lo, 1)

            for m in range(2 * STEPS):
                split_lo(0, m)
            with pool.Fori(1, NBLK // 2) as i:
                for m in range(2 * STEPS):
                    split_lo(i, m)

            def past_of(g):
                for h in range(HG):
                    n = HG * g + h
                    pool.wait_ge(x3_turned[h], 32 * (g + 1))
                    at_least(pool, c3_past, n - 1)
                    nc.gpsimd.tensor_tensor(past[:, h % 2].rearrange("p (k t) -> p k t", k=NBLK), x3t[:, h, 0, :, ::-1],
                                            x3t[:, h, 1, :, ::-1], ALU.add).then_inc(past_summed, 1)
                    pool.wait_ge(past_summed, n + 1)
                    nc.gpsimd.tensor_tensor(past[:, h % 2], past[:, h % 2], one_xs[:, :].to_broadcast([P, T]),
                                            ALU.mult).then_inc(past_ready, 1)

            pool.wait_ge(zeros_ready, 2)
            past_of(0)
            with pool.Fori(1, NG) as g:
                past_of(g)

        @block.tensor
        def _(pe):
            for n in range(16):
                dgroup, part = n // 2, n % 2
                if n % 8 == 0:
                    pe.wait_ge(w0_hi, n // 8 + 1)
                    pe.wait_ge(w0_lo, n // 8 + 1)
                at_least(pe, (pick_hi_copied, pick_lo_copied)[part], dgroup - 3)
                src = (w0h, w0l)[part][0:NID, :].rearrange("i (c d) -> i d c", d=C)
                for e in range(8):
                    for q in range(2):
                        mm = nc.tensor.matmul(ps[q * C:(q + 1) * C, n % 8, e * PAIRS:(e + 1) * PAIRS], src[:, 8 * dgroup + e, :],
                                              onehot[:, :].rearrange("i (n q) -> i q n", q=2)[:, q, :], start=True, stop=True)
                mm.then_inc(pick_summed, 1)
            pe.wait_ge(pick_hi_copied, 8)
            pe.wait_ge(pick_lo_copied, 8)

            def turn_params():
                pe.wait_ge(params_ready, 1)
                nc.tensor.transpose(ps[:, 5, 0:NBLK], bias_rev[0:NBLK, :], ident[0:NBLK, 0:NBLK])
                for n in range(4):
                    mm = nc.tensor.transpose(ps[:, 4, n * P:(n + 1) * P], prm[:, 1024 + n * P:1024 + (n + 1) * P], ident[:, :])
                mm.then_inc(params_turned, 1)

            def sum_k(c):
                pe.wait_ge(tables_ready, c + 1)
                if isinstance(c, int) and c == 0:
                    pe.wait_ge(turned_copied, 1)
                at_least(pe, k_scaled, c)
                for h in range(CH):
                    mm = nc.tensor.matmul(ps[0:TB, 4, h * TB:(h + 1) * TB], turn_own[:, h * TB:(h + 1) * TB],
                                          turn_r[:, h * TB:(h + 1) * TB], start=True, stop=True)
                mm.then_inc(k_summed, 1)

            def turn_lot(n):
                pe.wait_ge(w2_ready, n + 1)
                at_least(pe, w2_hi, n)
                at_least(pe, w2_lo, n)
                for m in range(NBLK):
                    mm = nc.tensor.transpose(ps[:, 6 + m // 4, (m % 4) * P:(m % 4 + 1) * P], wrow_rev[:, m * P:(m + 1) * P],
                                             ident[:, :])
                mm.then_inc(w2_turned, 1)

            def stage0(i, first):
                for m in range(2 * STEPS):
                    n = 2 * STEPS * i + m
                    s = m % NXH
                    k, step, odd = m // STEPS, m % STEPS // 2, m % 2
                    blk = 2 * i + k
                    pe.wait_ge(x_hi, n + 1)
                    pe.wait_ge(x_lo, n + 1)
                    at_least(pe, (s0_even_out, s0_odd_out)[odd], STEPS * i + m // 2 - 1)
                    for j in range(GPAIRS):
                        o = ps[:, s, j * P:(j + 1) * P]
                        w = pick[:, (m % STEPS) * GPAIRS + j]
                        nc.tensor.matmul(o, xh[:, s, j, :], w[:, 0, :], start=True, stop=False)
                        nc.tensor.matmul(o, xh[:, s, j, :], w[:, 1, :], start=False, stop=False)
                        mm = nc.tensor.matmul(o, xl[:, s, j, :], w[:, 0, :], start=False, stop=True)
                    mm.then_inc(s0_summed, 1)
                    if not odd:
                        continue
                    if first and k == 0:
                        if step == 0:
                            turn_lot(LOT_B)
                        if step == 3:
                            turn_lot(LOT_A)
                        if step == 5:
                            turn_lot(LOT_W)
                    else:
                        if step == 1:
                            sum_k(blk - 1)
                        if step == 5:
                            turn_lot(blk + LOT_W)

            pe.wait_ge(iota_done, 7)
            turn_params()
            stage0(0, True)
            with pe.Fori(1, NBLK // 2) as i:
                stage0(i, False)
            sum_k(NBLK - 1)

            pe.wait_ge(s0_even_out, NBLK * STEPS // 2)
            pe.wait_ge(s0_odd_out, NBLK * STEPS // 2)

            def conv1(g, h):
                n = HG * g + h
                b0 = 2 * (h % 2)
                pe.wait_ge(g1_turned, n + 1)
                pe.wait_ge(x1_hi, n + 1)
                pe.wait_ge(x1_lo, n + 1)
                if h < 2:
                    at_least(pe, c3_out, HG * (g - 1))
                else:
                    pe.wait_ge(c1_out, n - 1)
                products = [(0, x1h), (0, x1l), (1, x1h)]
                for d in range(NBLK):
                    for q, (part, xx) in enumerate(products):
                        w = g1[:, h, part, d * P:(d + 1) * P]
                        first, last = d == 0 and q == 0, q == 2
                        if d < 4:
                            nc.tensor.matmul(ps[:, b0, d * B:4 * B], w, xx[:, h, 0:4 - d, :],
                                             start=first, stop=(d == 3 and last))
                        lo = max(0, 4 - d)
                        mm = nc.tensor.matmul(ps[:, b0 + 1, (lo + d - 4) * B:4 * B], w, xx[:, h, lo:NBLK - d, :],
                                              start=first, stop=(d == NBLK - 1 and last))
                mm.then_inc(c1_summed, 1)

            def stage2(g):
                pe.wait_ge(x2_hi, HG * (g + 1))
                pe.wait_ge(x2_lo, HG * (g + 1))
                products = [(0, x2h), (0, x2l), (1, x2h)]
                for k in range(NBLK):
                    for q, (part, xx) in enumerate(products):
                        mm = nc.tensor.matmul(ps[:, 7, :], at[:, part, k, :], xx[:, :, k, :],
                                              start=(k == 0 and q == 0), stop=(k == NBLK - 1 and q == 2))
                mm.then_inc(low_summed, 1)
                for o in range(NBLK):
                    if o >= 3:
                        pe.wait_ge(s2_out, NBLK * g + o - 2)
                    for k in range(NBLK):
                        for q, (part, xx) in enumerate(products):
                            nc.tensor.matmul(ps[:, 4 + o % 3, :], w2t[:, part, k, o * P:(o + 1) * P], xx[:, :, k, :],
                                             start=(k == 0 and q == 0), stop=False)
                    if o == 0:
                        pe.wait_ge(low_hi, g + 1)
                        pe.wait_ge(low_lo, g + 1)
                    for q, (part, xx) in enumerate([(0, lowh), (0, lowl), (1, lowh)]):
                        mm = nc.tensor.matmul(ps[:, 4 + o % 3, :], bt[:, part, o * P:(o + 1) * P], xx, start=False, stop=(q == 2))
                    mm.then_inc(s2_summed, 1)

            def conv3(g, h):
                n = HG * g + h
                b0 = 2 * (h % 2)
                pe.wait_ge(g3_loaded[h], 16 * (g + 1))
                if h == 0:
                    pe.wait_ge(x3_hi, NBLK * (g + 1))
                    pe.wait_ge(x3_lo, NBLK * (g + 1))
                if h < 2:
                    pe.wait_ge(c1_out, conv1_sums_read(g, h))
                else:
                    pe.wait_ge(c3_out, n - 1)
                for j in range(NBLK):
                    for xx, parts in ((x3h, (0, 1)), (x3l, (0,))):
                        w = xx[:, h, j, :]
                        for part in parts:
                            first = j == 0 and xx is x3h and part == 0
                            last = xx is x3l
                            if j < 4:
                                nc.tensor.matmul(ps[:, b0, j * P:512], w, g3[:, h, part, 0:512 - j * P],
                                                 start=first, stop=(j == 3 and last))
                            c0 = max(0, 512 - j * P)
                            mm = nc.tensor.matmul(ps[:, b0 + 1, max(0, j * P - 512):512], w, g3[:, h, part, c0:T - j * P],
                                                  start=first, stop=(j == NBLK - 1 and last))
                mm.then_inc(c3_summed, 1)

            def conv1_sums_read(g, h):
                if isinstance(g, int) and g == NG - 1:
                    return HG * NG
                return HG * (g + 1) + 3 + h

            for h in range(HG):
                conv1(0, h)

            pe.wait_ge(k_scaled, NBLK)
            pe.wait_ge(w2_hi, LOT_W + NBLK)
            pe.wait_ge(w2_lo, LOT_W + NBLK)

            def body(g, more1):
                stage2(g)
                if more1:
                    for h in range(HG):
                        conv1(g + 1, h)
                for h in range(HG):
                    conv3(g, h)

            body(0, True)
            with pe.Fori(1, NG - 2) as g:
                body(g, True)
            body(NG - 2, True)
            body(NG - 1, False)

        @block.scalar
        def _(act):
            def load_lot(n):
                at_least(act, w2_ready, n)
                if isinstance(n, int) and n == LOT_B:
                    for a in range(NADAPT):
                        act.dma_start(wrow.rearrange("p (k a r) -> p k a r", k=NBLK, a=NADAPT)[:, :, a, :],
                                      lora_b[a].rearrange("(k o) r -> o k r", k=NBLK)).then_inc(wrow_loaded, 16)
                elif isinstance(n, int) and n == LOT_A:
                    act.dma_start(wrow, lora_a.rearrange("a r i -> (a r) i")).then_inc(wrow_loaded, 16)
                else:
                    act.dma_start(wrow, w2[bass.ds((n - LOT_W) * P, P), :]).then_inc(wrow_loaded, 16)

            def store_k(c):
                act.wait_ge(k_split, c + 1)
                rows = krow.rearrange("v h s n -> (v h) s n")[bass.ds(c * CH, CH)]
                for part, half in enumerate((kh, kl)):
                    act.dma_start(rows[:, part, P:].rearrange("h (a b) -> a h b", a=TB),
                                  half[0:TB, :].rearrange("a (h b) -> a h b", h=CH)).then_inc(krow_stored, 16)

            for v in range(2):
                rows = slice(v * C, (v + 1) * C)
                log_dt, cc, log_ar, a_imag, dd = ssm[v]
                act.dma_start(prm[rows, 63:64], log_dt.rearrange("(h o) -> h o", o=1)).then_inc(ssm_loaded, 16)
                act.dma_start(prm[rows, 64:128], log_ar).then_inc(ssm_loaded, 16)
                act.dma_start(prm[rows, 128:192], a_imag).then_inc(ssm_loaded, 16)
                act.dma_start(prm[rows, 192:320], cc.rearrange("h n r -> h (n r)")).then_inc(ssm_loaded, 16)
                act.dma_start(prm[0:1, 320 + v * C:320 + (v + 1) * C], dd.rearrange("(o h) -> o h", o=1)).then_inc(ssm_loaded, 16)
            load_lot(LOT_B)
            for a in range(NADAPT):
                act.dma_start(rank_scale[a * RANK:(a + 1) * RANK, :],
                              lora_s[a:a + 1].rearrange("(o a) -> o a", o=1).to_broadcast([RANK, 1])).then_inc(consts_loaded, 16)
            act.dma_start(biasn[0:NBLK, :], bias2.rearrange("(k o) -> k o", k=NBLK)).then_inc(consts_loaded, 16)
            act.wait_ge(zeros_ready, 1)
            act.dma_start(krow.rearrange("v h s n -> (v h) s n")[:, :, 0:P],
                          zrow[:, :].bitcast(F16).rearrange("p (s n) -> p s n", s=2)).then_inc(krow_stored, 16)

            act.wait_ge(angles_ready, 1)
            nc.scalar.activation(prm[:, 704:832], prm[:, 704:832], ACT.Sin).then_inc(sines_ready, 1)
            nc.scalar.activation(prm[:, 832:896], prm[:, 512:576], ACT.Tanh, scale=0.5).then_inc(sines_ready, 1)

            act.wait_ge(w0_ready, 1)
            for half in range(2):
                nc.scalar.activation(half_cols(w0h, half), half_cols(w0n, half), ACT.Copy, scale=FS).then_inc(w0_hi, 1)
            act.wait_ge(pick_cleared, 1)
            for dgroup in range(8):
                act.wait_ge(pick_summed, 2 * dgroup + 1)
                for q in range(2):
                    rows = slice(q * C, (q + 1) * C)
                    e = nc.scalar.activation(pick[rows, :, 0, q * C + 8 * dgroup:q * C + 8 * dgroup + 8],
                                             ps[rows, 2 * dgroup % 8, :].rearrange("p (e n) -> p n e", e=8), ACT.Copy)
                e.then_inc(pick_hi_copied, 1)

            def copy_turned():
                act.wait_ge(params_turned, 1)
                nc.scalar.activation(turned.rearrange("p n r -> p (n r)"), ps[:, 4, :], ACT.Copy).then_inc(turned_copied, 1)

            def chunk_sines(c, step):
                if step == 3:
                    act.wait_ge(table_angles, 2 * c + 1)
                    nc.scalar.activation(turn_r, turn_r, ACT.Sin, bias=phase_own, scale=-TURN)
                if step == 4:
                    act.wait_ge(table_step, NLINK * c + 8)
                    nc.scalar.activation(turn_own, turn_own, ACT.Sin, bias=phase_own, scale=-TURN)
                if step == 5:
                    act.wait_ge(table_angles, 2 * c + 2)
                    nc.scalar.activation(turn_oth, turn_oth, ACT.Sin, bias=phase_oth, scale=-TURN)
                if step == 6:
                    nc.scalar.activation(angle_r, angle_r, ACT.Exp)
                    nc.scalar.activation(angle_l, angle_l, ACT.Exp).then_inc(table_sines, 1)

            def scale_k(c):
                act.wait_ge(k_summed, c + 1)
                nc.scalar.activation(kf[0:TB, :], ps[0:TB, 4, :], ACT.Copy, scale=WS).then_inc(k_scaled, 1)

            def lot_hi(n):
                act.wait_ge(w2_turned, n + 1)
                nc.scalar.activation(act_gate, pcol, ACT.Copy)
                nc.scalar.activation(lot_target(n, 0), turned_tiles(n), ACT.Copy,
                                     scale=WS).then_inc(w2_hi, 1)

            def split_hi(i, m):
                n = 2 * STEPS * i + m
                act.wait_ge(x_loaded[m % NXIN], 16 * (2 * STEPS // NXIN * i + m // NXIN + 1))
                at_least(act, s0_summed, n - NXH + 1)
                nc.scalar.activation(xh[:, m % NXH, :, ::-1], xin[:, m % NXIN], ACT.Copy).then_inc(x_hi, 1)

            def copy_even(i, m):
                k, g = m // STEPS, m % STEPS
                if g == 0:
                    for part in range(NPART):
                        at_least(act, x1_stored[k][part], 16 * i)
                    at_least(act, x1_kept, 2 * i + k - 1)
                act.wait_ge(s0_summed, 2 * STEPS * i + m + 1)
                nc.scalar.activation(xq[:, k, :, 2 * GPAIRS * g:2 * GPAIRS * (g + 1)],
                                     ps[:, m % NXH, :].rearrange("p (b d) -> p d b", d=C), ACT.Copy).then_inc(s0_even_out, 1)

            def stage0(i, first):
                for m in range(2 * STEPS):
                    k, step = m // STEPS, m % STEPS // 2
                    blk = 2 * i + k
                    split_hi(i, m)
                    if m % 2 == 0:
                        continue
                    if m >= 3:
                        copy_even(i, m - 3)
                    elif not first:
                        copy_even(i - 1, 2 * STEPS - 2)
                    if first and k == 0:
                        if step == 0:
                            copy_turned()
                        if step == 1:
                            load_lot(LOT_A)
                            lot_hi(LOT_B)
                        if step == 3:
                            load_lot(LOT_W)
                        if step == 4:
                            lot_hi(LOT_A)
                        if step == 6:
                            lot_hi(LOT_W)
                    else:
                        if step == 0:
                            load_lot(blk + LOT_W)
                        if step == 2:
                            scale_k(blk - 1)
                        if step == 7:
                            store_k(blk - 1)
                            lot_hi(blk + LOT_W)
                    chunk_sines(blk, step)

            stage0(0, True)
            with act.Fori(1, NBLK // 2) as i:
                stage0(i, False)
            copy_even(NBLK // 2 - 1, 2 * STEPS - 2)

            def x1_split_hi(g, h):
                if isinstance(g, int) and g == 0:
                    act.wait_ge(x1_kept, NBLK)
                else:
                    act.wait_ge(x1_loaded[h], 16 * g)
                nc.scalar.activation(x1h[:, h], x1f[:, h], ACT.Copy, scale=XS / FS).then_inc(x1_hi, 1)

            def x2_split_hi(g, h):
                act.wait_ge(c1_out, HG * g + h + 1)
                nc.scalar.activation(x2h[:, h], x1f[:, h], ACT.Copy, scale=XS / FS).then_inc(x2_hi, 1)

            for h in range(HG):
                x1_split_hi(0, h)
                if h == 0:
                    scale_k(NBLK - 1)
            store_k(NBLK - 1)
            for h in range(HG):
                x2_split_hi(0, h)
            for h in range(HG):
                x1_split_hi(1, h)

            def body(g, more1, more2):
                act.wait_ge(low_scaled, g + 1)
                nc.scalar.activation(lowh.rearrange("p (h b) -> p h b", h=HG), lowf, ACT.Copy).then_inc(low_hi, 1)
                for h in range(HG):
                    at_least(act, x3_turned[h], 32 * g)
                for o in range(NBLK):
                    act.wait_ge(s2_summed, NBLK * g + o + 1)
                    nc.scalar.activation(x3h[:, :, o, :], ps[:, 4 + o % 3, :].rearrange("p (h b) -> p h b", h=HG), ACT.Identity,
                                         bias=biasx[:, o:o + 1], scale=XS / FS).then_inc(x3_hi, 1)
                if more1:
                    for h in range(HG):
                        x2_split_hi(g + 1, h)
                for h in range(HG):
                    act.wait_ge(c3_summed, HG * g + h + 1)
                    at_least(act, out_stored[h], 16 * g)
                    nc.scalar.activation(outt[:, h].rearrange("p (n c) -> p n c", n=2), ps[:, 2 * (h % 2):2 * (h % 2) + 2, :],
                                         ACT.Copy, scale=1.0 / FS).then_inc(c3_out, 1)
                    if more2:
                        x1_split_hi(g + 2, h)

            body(0, True, True)
            with act.Fori(1, NG - 2) as g:
                body(g, True, True)
            body(NG - 2, True, False)
            body(NG - 1, False, False)

        @block.vector
        def _(dve):
            step = [0]

            def link(ins):
                step[0] += 1
                ins.then_inc(dve_step, 1)
                dve.wait_ge(dve_step, step[0])

            ts, tt, stt = nc.vector.tensor_scalar, nc.vector.tensor_tensor, nc.vector.scalar_tensor_tensor

            dve.wait_ge(iota_done, 3)
            dve.wait_ge(ids_loaded, 64)
            nc.vector.tensor_copy(idf[:, :, :], ids[:, :, :])
            link(nc.vector.tensor_copy(pcol, pcoli))
            ts(onehot[:, :], idf[0:NID, 0, :], pcol[0:NID, :], None, ALU.is_equal)
            nc.vector.tensor_copy(tcol, tcoli)
            nc.vector.tensor_copy(trow[:, :], trowi[:, :])
            link(nc.vector.tensor_copy(len3f, len3i))
            nc.vector.tensor_copy(steps[:, 0:TB], trow[:, 0:TB])
            nc.vector.tensor_copy(steps[:, TB:2 * TB], trow.rearrange("p (l s) -> p l s", s=TB)[:, :, 0])
            for k in range(NBLK):
                ts(mask1[:, k, :], idf[:, 1, :], tcol[:, k:k + 1], None, ALU.is_gt).then_inc(masks_ready, 1)
            ts(past3[:, :], trow[:, :], len3f, None, ALU.is_ge).then_inc(masks_ready, 1)

            def col(n, w=64):
                return prm[:, 64 * n:64 * n + w]

            def exp_exact(dst, src, t1, t2, t3):
                link(ts(t1, src, 1.0 / math.log(2.0), ROUND, ALU.mult, ALU.add))
                link(ts(t1, t1, ROUND, -126.0, ALU.subtract, ALU.max))
                link(stt(t2, t1, -LN2_HI, src, ALU.mult, ALU.add))
                link(stt(t2, t1, -LN2_LO, t2, ALU.mult, ALU.add))
                link(ts(t3, t2, 1.0 / 5040, None, ALU.mult))
                for c in (720, 120, 24, 6, 2, 1):
                    link(stt(t3, t3, 1.0 / c, t2, ALU.add, ALU.mult))
                link(ts(t3, t3, 1.0, None, ALU.add))
                link(ts(t1.bitcast(I32), t1, 127.0, 8388608.0, ALU.add, ALU.mult))
                link(tt(dst, t3, t1, ALU.mult))

            def turns(dst, src, tmp):
                link(ts(tmp, src, 1.0 / (2 * math.pi), None, ALU.mult))
                link(ts(tmp, tmp, ROUND, ROUND, ALU.add, ALU.subtract))
                link(stt(dst, tmp, -TWO_PI_HI, src, ALU.mult, ALU.add))
                link(stt(dst, tmp, -TWO_PI_LO, dst, ALU.mult, ALU.add))
                link(ts(dst, dst, PI_CLAMP, -PI_CLAMP, ALU.min, ALU.max))

            dt = prm[:, 1023:1024]
            t = [col(n) for n in range(16, 32)]
            ar, ai = t[0], col(2)
            re, im = col(8), col(9)

            dve.wait_ge(ssm_loaded, 160)
            exp_exact(prm[:, 1023:1088], prm[:, 63:128], *[prm[:, 128 * n:128 * n + 65] for n in (9, 10, 11)])
            link(ts(re, ar, dt, -1.0, ALU.mult, ALU.mult))
            link(ts(im, ai, dt, None, ALU.mult))
            link(ts(ar, ar, -1.0, None, ALU.mult))
            link(ts(col(10), im, 0.5, None, ALU.mult))
            turns(prm[:, 704:832], prm[:, 576:704], prm[:, 1856:1984])
            link(ts(col(14), col(11), 1.0 / (2 * math.pi), None, ALU.mult))
            exp_exact(t[6], re, t[1], t[2], t[3])
            tt(t[5], ar, ar, ALU.mult).then_inc(angles_ready, 1)
            link(tt(t[4], ai, ai, ALU.mult))
            link(tt(t[4], t[4], t[5], ALU.add))
            link(nc.vector.reciprocal(t[7], t[4]))

            dve.wait_ge(w0_loaded, 64)
            diag = w0n[0:NID, 0:C * C]
            diag = bass.AP(diag.tensor, diag.offset, [diag.ap[0], [C + 1, C]])
            ts(diag, diag, 1.0, None, ALU.add).then_inc(w0_ready, 1)

            link(ts(rank_adapter, pcol, 1.0 / RANK, -0.5 + 0.5 / RANK, ALU.mult, ALU.add))
            link(ts(rank_adapter, rank_adapter, ROUND, ROUND, ALU.add, ALU.subtract))
            dve.wait_ge(consts_loaded, 16 * (NADAPT + 1))
            link(ts(rank_scale, rank_scale, XS / FS, None, ALU.mult))
            ts(adapter_scale[:, :], idf[:, 2, :], rank_adapter, rank_scale, ALU.is_equal, ALU.mult)
            nc.vector.tensor_copy(bias_rev[0:NBLK, ::-1], biasn[0:NBLK, :])
            link(ts(quarter_own, pcol, float(C), 0.25, ALU.is_lt, ALU.mult))
            link(ts(quarter_oth, quarter_own, -1.0, 0.25, ALU.mult, ALU.add))
            for n, (half, quarter) in enumerate(((half_own, quarter_own), (half_oth, quarter_oth))):
                ts(half[:, 0:1], quarter, 0.5, None, ALU.subtract)
                ts(half[:, 1:2], quarter, 0.5, None, ALU.add)
            link(ts(phase_own, quarter_own, 2 * math.pi, None, ALU.mult))
            link(ts(phase_oth, quarter_oth, 2 * math.pi, None, ALU.mult))
            for half in range(2):
                dve.wait_ge(w0_hi, half + 1)
                stt(half_cols(w0l, half), half_cols(w0n, half), FS, half_cols(w0h, half), ALU.mult, ALU.subtract).then_inc(w0_lo, 1)

            dve.wait_ge(sines_ready, 2)
            sin, sinh2, tanh = col(11), col(12), col(13)
            link(ts(t[1], t[6], 1.0, None, ALU.add))
            link(tt(t[1], t[1], tanh, ALU.mult))
            link(tt(t[2], sinh2, sinh2, ALU.mult))
            link(ts(t[5], t[2], -2.0, 1.0, ALU.mult, ALU.add))
            link(tt(t[1], t[1], t[5], ALU.mult))
            link(stt(t[1], t[2], -2.0, t[1], ALU.mult, ALU.add))
            link(tt(t[2], t[6], sin, ALU.mult))
            cr = prm[:, 192:320].rearrange("p (n r) -> p r n", r=2)[:, 0, :]
            ci = prm[:, 192:320].rearrange("p (n r) -> p r n", r=2)[:, 1, :]

            def complex_mult(o_re, o_im, a_re, a_im, b_re, b_im, t1):
                link(tt(o_re, a_re, b_re, ALU.mult))
                link(tt(t1, a_im, b_im, ALU.mult))
                link(tt(o_re, o_re, t1, ALU.subtract))
                link(tt(o_im, a_re, b_im, ALU.mult))
                link(tt(t1, a_im, b_re, ALU.mult))
                link(tt(o_im, o_im, t1, ALU.add))

            complex_mult(t[8], t[9], cr, ci, t[1], t[2], t[3])
            link(ts(t[10], ai, -1.0, None, ALU.mult))
            complex_mult(t[11], t[12], t[8], t[9], ar, t[10], t[3])
            link(tt(t[11], t[11], t[7], ALU.mult))
            link(tt(t[12], t[12], t[7], ALU.mult))
            big = prm[:, 1024:1536]
            nc.vector.tensor_copy(big[:, 0:64], re)
            nc.vector.tensor_copy(big[:, 64:128], re)
            nc.vector.tensor_copy(big[:, 128:192], col(14))
            nc.vector.tensor_copy(big[:, 192:256], col(14))
            ts(big[:, 256:320], t[11], 2.0, None, ALU.mult)
            ts(big[:, 320:384], t[11], -2.0, None, ALU.mult)
            ts(big[:, 384:448], t[12], -2.0, None, ALU.mult)
            ts(big[:, 448:512], t[12], -2.0, None, ALU.mult)
            ts(d_row[0:1, :], prm[0:1, 320:448], 1.0, WS, ALU.add, ALU.mult).then_inc(params_ready, 1)

            dve.wait_ge(pick_cleared, 1)
            for dgroup in range(8):
                dve.wait_ge(pick_summed, 2 * dgroup + 2)
                for q in range(2):
                    rows = slice(q * C, (q + 1) * C)
                    e = nc.vector.tensor_copy(pick[rows, :, 1, q * C + 8 * dgroup:q * C + 8 * dgroup + 8],
                                              ps[rows, (2 * dgroup + 1) % 8, :].rearrange("p (e n) -> p n e", e=8))
                e.then_inc(pick_lo_copied, 1)

            right_l = steps[:, 0:TB].rearrange("p (o l) -> p o l", o=1).to_broadcast([P, CH, TB])
            left_l = steps[:, TB:2 * TB].rearrange("p (o l) -> p o l", o=1).to_broadcast([P, CH, TB])

            def table_link(ins, c, n):
                ins.then_inc(table_step, 1)
                dve.wait_ge(table_step, NLINK * c + n)

            def param(c, n):
                return turned[:, n, bass.ds(c * CH, CH)].rearrange("p (h o) -> p h o", o=1).to_broadcast([P, CH, TB])

            def round_off(tile, angle, quarter, half, c, n):
                table_link(ts(tile, angle, quarter, ROUND, ALU.add, ALU.add), c, n)
                table_link(stt(tile, tile, ROUND, angle, ALU.subtract, ALU.subtract), c, n + 1)
                table_link(ts(tile, tile, half[:, 0:1], half[:, 1:2], ALU.max, ALU.min), c, n + 2)

            def right_angles(c):
                at_least(dve, k_summed, c)
                table_link(tt(wide(angle_r), param(c, 1), right_l, ALU.mult), c, 1)
                round_off(turn_r, angle_r, quarter_own, half_own, c, 2)
                tt(wide(angle_r), param(c, 0), right_l, ALU.mult).then_inc(table_angles, 1)

            def left_angles(c):
                table_link(tt(wide(angle_l), param(c, 1), left_l, ALU.mult), c, 5)
                round_off(turn_own, angle_l, quarter_own, half_own, c, 6)

            def other_angles(c):
                round_off(turn_oth, angle_l, quarter_oth, half_oth, c, 9)
                tt(wide(angle_l), param(c, 0), left_l, ALU.mult).then_inc(table_angles, 1)

            def combine(c):
                dve.wait_ge(table_sines, c + 1)
                table_link(tt(turn_r, turn_r, angle_r, ALU.mult), c, 12)
                table_link(tt(wide(turn_own), wide(turn_own), param(c, 2), ALU.mult), c, 13)
                table_link(tt(wide(turn_oth), wide(turn_oth), param(c, 3), ALU.mult), c, 14)
                table_link(tt(turn_own, turn_own, turn_oth, ALU.add), c, 15)
                tt(turn_own, turn_own, angle_l, ALU.mult).then_inc(tables_ready, 1)

            def split_k(c):
                dve.wait_ge(k_scaled, c + 1)
                dve.wait_ge(krow_stored, 32 * c + 16)
                k0 = wide(kf)[0:1, :, 0]
                tt(k0, k0, d_row[0:1, bass.ds(c * CH, CH)], ALU.add).then_inc(d_added, 1)
                dve.wait_ge(d_added, c + 1)
                nc.vector.tensor_copy(kh[0:TB, :], kf[0:TB, :]).then_inc(k_hi, 1)
                dve.wait_ge(k_hi, c + 1)
                tt(kl[0:TB, :], kf[0:TB, :], kh[0:TB, :], ALU.subtract).then_inc(k_split, 1)

            def lot_ready(n):
                dve.wait_ge(wrow_loaded, 16 * (NADAPT + n))
                at_least(dve, w2_turned, n)
                src = wrow.rearrange("p (m i) -> p m i", m=NBLK)
                dst = wrow_rev.rearrange("p (m i) -> p m i", m=NBLK)
                if isinstance(n, int) and n == LOT_B:
                    nc.vector.tensor_copy(wrow_rev, wrow).then_inc(w2_ready, 1)
                elif isinstance(n, int) and n == LOT_A:
                    nc.vector.tensor_copy(dst[:, :, ::-1], src).then_inc(w2_ready, 1)
                else:
                    nc.vector.tensor_copy(dst[:, :, ::-1], src).then_inc(w2_rev, 1)
                    dve.wait_ge(w2_rev, n - LOT_W + 1)
                    own = wrow_rev[:, bass.ds((n - LOT_W) * P, P)]
                    stt(own, flip[:, :], XS, own, ALU.mult, ALU.add).then_inc(w2_ready, 1)

            def lot_lo(n):
                dve.wait_ge(w2_hi, n + 1)
                stt(lot_target(n, 1), turned_tiles(n), WS, lot_target(n, 0),
                    ALU.mult, ALU.subtract).then_inc(w2_lo, 1)

            def copy_odd(i, m):
                k, g = m // STEPS, m % STEPS
                if g == 1:
                    for part in range(NPART):
                        at_least(dve, x1_stored[k][part], 16 * i)
                dve.wait_ge(s0_summed, 2 * STEPS * i + m + 1)
                nc.vector.tensor_copy(xq[:, k, :, 2 * GPAIRS * g:2 * GPAIRS * (g + 1)],
                                      ps[:, m % NXH, :].rearrange("p (b d) -> p d b", d=C)).then_inc(s0_odd_out, 1)

            def keep_x1(i, k):
                blk = 2 * i + k
                dve.wait_ge(s0_even_out, (blk + 1) * (STEPS // 2))
                dve.wait_ge(s0_odd_out, (blk + 1) * (STEPS // 2))
                ts(x1f[:, :, bass.ds(blk, 1), :].rearrange("p h o b -> p (h o) b"), xq[:, k, 0:HG, :], 1.0, None,
                   ALU.mult).then_inc(x1_kept, 1)

            def turned_bias():
                dve.wait_ge(params_turned, 1)
                ts(biasx[:, :], ps[:, 5, 0:NBLK], XS, None, ALU.mult)
                dve.wait_ge(turned_copied, 1)

            def stage0(i, first):
                for m in range(1, 2 * STEPS, 2):
                    k, step = m // STEPS, m % STEPS // 2
                    blk = 2 * i + k
                    if m >= 3:
                        copy_odd(i, m - 2)
                    elif not first:
                        copy_odd(i - 1, 2 * STEPS - 1)
                    if step == 1 and not (first and k == 0):
                        keep_x1(*((i, 0) if k else (i - 1, 1)))
                    if first and k == 0:
                        if step == 0:
                            lot_ready(LOT_B)
                            turned_bias()
                        if step == 2:
                            lot_ready(LOT_A)
                            lot_lo(LOT_B)
                        if step == 4:
                            lot_ready(LOT_W)
                        if step == 5:
                            lot_lo(LOT_A)
                        if step == 7:
                            lot_lo(LOT_W)
                    else:
                        if step == 0:
                            combine(blk - 1)
                        if step == 1 and not (first and blk == 1):
                            lot_lo(blk - 1 + LOT_W)
                        if step == 5:
                            lot_ready(blk + LOT_W)
                        if step == 6:
                            split_k(blk - 1)
                    if step == 2:
                        right_angles(blk)
                    if step == 3:
                        left_angles(blk)
                    if step == 4:
                        other_angles(blk)

            stage0(0, True)
            with dve.Fori(1, NBLK // 2) as i:
                stage0(i, False)
            combine(NBLK - 1)
            copy_odd(NBLK // 2 - 1, 2 * STEPS - 1)
            keep_x1(NBLK // 2 - 1, 1)

            def turn_g1(g, h):
                dve.wait_ge(g1_loaded[h], 16 * (g + 1))
                at_least(dve, c1_summed, HG * (g - 1) + h + 1)
                if isinstance(g, int) and g == 0 and h == 0:
                    dve.wait_ge(k_summed, NBLK)
                if isinstance(g, int) and g == 0 and h == HG - 1:
                    dve.wait_ge(krow_stored, 16 + 32 * NBLK)
                nc.vector.tensor_copy(g1[:, h].rearrange("p s (d t) -> p (s d) t", t=P)[:, :, ::-1],
                                      g1n[:, h % 2].rearrange("p s (d t) -> p (s d) t", t=P)).then_inc(g1_turned, 1)

            gate = small[:, 40:40 + 2 * HG]
            dve.wait_ge(masks_ready, NBLK + 1)
            def x1_split_lo(g, h):
                dve.wait_ge(x1_hi, HG * g + h + 1)
                stt(x1l[:, h], x1f[:, h], XS / FS, x1h[:, h], ALU.mult, ALU.subtract).then_inc(x1_lo, 1)

            def take_conv1(g, h):
                dve.wait_ge(c1_summed, HG * g + h + 1)
                nc.vector.memset(gate[:, h:h + 1], 0.0)
                b0 = 2 * (h % 2)
                nc.vector.copy_predicated(x1f[:, h].rearrange("p k b -> p (k b)"), mask1[:, :, :].rearrange("p k b -> p (k b)"),
                                          ps[:, b0:b0 + 2, :].rearrange("p n c -> p (n c)")).then_inc(c1_out, 1)

            def x2_split_lo(g, h):
                dve.wait_ge(x2_hi, HG * g + h + 1)
                stt(x2l[:, h], x1f[:, h], XS / FS, x2h[:, h], ALU.mult, ALU.subtract).then_inc(x2_lo, 1)

            def conv1(g):
                for h in range(HG):
                    take_conv1(g, h)
                    if h:
                        x2_split_lo(g, h - 1)
                x2_split_lo(g, HG - 1)

            for h in range(HG):
                x1_split_lo(0, h)
                if h == 0:
                    lot_lo(NBLK - 1 + LOT_W)
                if h == 2:
                    split_k(NBLK - 1)
                turn_g1(0, h)
            conv1(0)
            for h in range(HG):
                turn_g1(1, h)
                x1_split_lo(1, h)

            def body(g, more1, more2):
                dve.wait_ge(low_summed, g + 1)
                tt(lowf, ps[:, 7, :].rearrange("p (h b) -> p h b", h=HG),
                   adapter_scale[:, :].rearrange("p (o b) -> p o b", o=1).to_broadcast([P, HG, B]), ALU.mult).then_inc(low_scaled, 1)
                dve.wait_ge(low_hi, g + 1)
                tt(lowl.rearrange("p (h b) -> p h b", h=HG), lowf, lowh.rearrange("p (h b) -> p h b", h=HG),
                   ALU.subtract).then_inc(low_lo, 1)

                for h in range(HG):
                    at_least(dve, x3_turned[h], 32 * g)

                def lo3(o):
                    dve.wait_ge(s2_out, NBLK * g + o + 1)
                    tt(x3l[:, :, o, :], x3f[:, o % 2], x3h[:, :, o, :], ALU.subtract).then_inc(x3_lo, 1)

                for o in range(NBLK):
                    if o >= 2:
                        dve.wait_ge(x3_lo, NBLK * g + o - 1)
                    dve.wait_ge(x3_hi, NBLK * g + o + 1)
                    ts(x3f[:, o % 2], ps[:, 4 + o % 3, :].rearrange("p (h b) -> p h b", h=HG), XS / FS, biasx[:, o:o + 1],
                       ALU.mult, ALU.add).then_inc(s2_out, 1)
                    if o:
                        lo3(o - 1)
                lo3(NBLK - 1)
                if more1:
                    conv1(g + 1)
                for h in range(HG):
                    dve.wait_ge(c3_out, HG * g + h + 1)
                    dve.wait_ge(past_ready, HG * g + h + 1)
                    nc.vector.memset(gate[:, HG + h:HG + h + 1], 0.0)
                    nc.vector.copy_predicated(outt[:, h], past3[:, :], past[:, h % 2]).then_inc(c3_past, 1)
                    if more2:
                        turn_g1(g + 2, h)
                        x1_split_lo(g + 2, h)

            body(0, True, True)
            with dve.Fori(1, NG - 2) as g:
                body(g, True, True)
            body(NG - 2, True, False)
            body(NG - 1, False, False)


_INS = ['x', 'itok_B_0_15', 'itok_B_78_3631', 'itok_B_1_7', 'itok_B_8_3872', 'L0_cond_weights',
        'L1_cond_log_dt', 'L1_cond_C', 'L1_cond_log_A_real', 'L1_cond_A_imag', 'L1_cond_D',
        'L2_cond_weight', 'L2_cond_bias', 'L2_cond_lora_a_weights', 'L2_cond_lora_b_weights', 'L2_cond_scaling_factors',
        'L3_cond_log_dt', 'L3_cond_C', 'L3_cond_log_A_real', 'L3_cond_A_imag', 'L3_cond_D']


def kernel(**inputs):
    import numpy as _np
    import concourse.bacc as _bacc
    from concourse import mybir as _mybir
    from concourse.bass_utils import run_bass_kernel_spmd as _run

    nc = _bacc.Bacc("TRN2", target_bir_lowering=False, num_devices=1)
    arrays, ap = {}, {}
    for name in _INS:
        a = _np.ascontiguousarray(inputs[name])
        arrays[f"in_{name}_dram"] = a
        ap[name] = nc.dram_tensor(f"in_{name}_dram", a.shape, _mybir.dt.from_np(a.dtype), kind="ExternalInput").ap()
    out = nc.dram_tensor("out_0_dram", (B, C, T), _mybir.dt.float32, kind="ExternalOutput").ap()

    def ssm(p):
        return tuple(ap[f"{p}_cond_{n}"] for n in ("log_dt", "C", "log_A_real", "A_imag", "D"))

    build(nc, ap['x'], ap['itok_B_0_15'], ap['itok_B_78_3631'], ap['itok_B_1_7'], ap['itok_B_8_3872'],
          ap['L0_cond_weights'], ssm("L1"), ssm("L3"), ap['L2_cond_weight'], ap['L2_cond_bias'],
          ap['L2_cond_lora_a_weights'], ap['L2_cond_lora_b_weights'], ap['L2_cond_scaling_factors'], out)
    r = _run(nc, [arrays], core_ids=[0])
    return r.results[0]["out_0_dram"]
```
